# Optimizing a Trainium2 kernel written in Bass

```python
import numpy as np
import jax
import jax.numpy as jnp

def _softmax(x, axis=-1):
    return jax.nn.softmax(x, axis=axis)

def _gelu(x):
    return jax.nn.gelu(x, approximate=True)

def _silu(x):
    return jax.nn.silu(x)

def _sigmoid(x):
    return jax.nn.sigmoid(x)

def _layernorm(x, axis=-1, eps=1e-05):
    m = jnp.mean(x, axis=axis, keepdims=True)
    v = jnp.var(x, axis=axis, keepdims=True)
    return (x - m) / jnp.sqrt(v + eps)

def _scatter_add(tgt, idx, src, axis=0):
    return tgt.at[idx].add(src)

def _segment_sum(src, seg, n):
    return jax.ops.segment_sum(src, seg, n)
kernel_name = 'mk_xattn_ffn_d1_seqx_r4_43d380'

def setup_inputs(seed: int=0):
    np.random.seed(seed)
    _w = jnp.asarray

    def _rec_inputs():
        import jax
        import jax.numpy as jnp
        _rk = jax.random.key(seed)
        x = -7.109e-05 + 0.9999 * jax.random.normal(jax.random.fold_in(_rk, 1), (4, 512, 512), jnp.float32)
        _lenS = 512 - jax.random.randint(jax.random.fold_in(_rk, 7), (4,), 0, max(1, 512 // 4) + 1, jnp.int32)
        _lenS2 = 512 - jax.random.randint(jax.random.fold_in(_rk, 8), (4,), 0, max(1, 512 // 4) + 1, jnp.int32)
        _ctx_512P = jax.random.normal(jax.random.fold_in(_rk, 11), (4, 16, 128), jnp.float32)
        _ctx_512c = jax.random.dirichlet(jax.random.fold_in(_rk, 511), 0.3 * jnp.ones((16,), jnp.float32), (4, 512))
        _ctx_512t = jnp.einsum('bsk,bkd->bsd', _ctx_512c, _ctx_512P)
        _ctx_512t = _ctx_512t * jax.lax.rsqrt(jnp.mean(jnp.square(_ctx_512t)) + 1e-12) * 0.953939
        ctx_512 = 2.81802e-05 + 1.00001 * (_ctx_512t + 0.3 * jax.random.normal(jax.random.fold_in(_rk, 611), (4, 512, 128), jnp.float32))
        return (x, ctx_512)
    x, ctx_512 = _rec_inputs()

    def _L0_xattn_setup():
        import jax, jax.numpy as jnp
        import numpy as np
        EPS = 1e-06
        IMAGE_DIMS = 512
        key = jax.random.key(seed)
        k1, k2, k3 = jax.random.split(key, 3)
        B, I, J, D = (16, 512, 512, 128)
        p = jax.random.normal(k1, (B, I, J), dtype=jnp.float32)
        k_v = jax.random.normal(k2, (B, J, D), dtype=jnp.float32)
        W_k = jax.random.normal(k3, (D, D), dtype=jnp.float32) * (1.0 / np.sqrt(D))
        b_k = jnp.zeros((D,), dtype=jnp.float32)
        ln_gamma = jnp.ones((J,), dtype=jnp.float32)
        ln_beta = jnp.zeros((J,), dtype=jnp.float32)
        return {'p': p, 'k_v': k_v, 'W_k': W_k, 'b_k': b_k, 'ln_gamma': ln_gamma, 'ln_beta': ln_beta}
    _L0_xattn_all = _L0_xattn_setup()
    _L0_xattn_in = {k: v for k, v in _L0_xattn_all.items() if k in ('W_k', 'b_k', 'ln_gamma', 'ln_beta')}
    del _L0_xattn_all

    def _L0_ffn_setup():
        import jax, jax.numpy as jnp
        import numpy as np
        import math
        GOLDEN_CENTER = 1.0 / math.e
        GOLDEN_LOWER = 0.5 - math.log(4.0 / 3.0)
        GOLDEN_UPPER = 0.5
        B, T, D = (4, 256, 512)
        E = 8
        F = 2048 // (E // 2)
        R = 64
        NL = 2

        def _router_weights(x, Wr, temperature):
            logits = jnp.einsum('btd,de->bte', x, Wr)
            inhibition = jax.nn.sigmoid(logits / temperature)
            in_zone = (inhibition >= GOLDEN_LOWER) & (inhibition <= GOLDEN_UPPER)
            distance = jnp.abs(inhibition - GOLDEN_CENTER)
            w = jnp.exp(-distance / 0.1) * in_zone.astype(x.dtype)
            wsum = w.sum(axis=-1, keepdims=True)
            no_expert = wsum < 1e-08
            fb = jnp.exp(-distance / 0.3)
            _, top2 = jax.lax.top_k(fb, 2)
            fb_mask = jax.nn.one_hot(top2, E, dtype=x.dtype).sum(axis=-2)
            fb_w = fb * fb_mask
            fb_w = fb_w / jnp.clip(fb_w.sum(axis=-1, keepdims=True), 1e-08)
            w = jnp.where(no_expert, fb_w, w)
            return w / jnp.clip(w.sum(axis=-1, keepdims=True), 1e-08)
        key = jax.random.key(seed)
        ks = jax.random.split(key, 13)
        s = 0.02
        x = jax.random.normal(ks[0], (B, T, D), dtype=jnp.float32)
        Wg = jax.random.normal(ks[1], (E, D, F), dtype=jnp.float32) * s
        Wu = jax.random.normal(ks[2], (E, D, F), dtype=jnp.float32) * s
        Wd = jax.random.normal(ks[3], (E, F, D), dtype=jnp.float32) * s
        Ga = jax.random.normal(ks[4], (NL, D, R), dtype=jnp.float32) * s
        Gb = jax.random.normal(ks[5], (NL, R, F), dtype=jnp.float32) * s
        Ua = jax.random.normal(ks[6], (NL, D, R), dtype=jnp.float32) * s
        Ub = jax.random.normal(ks[7], (NL, R, F), dtype=jnp.float32) * s
        Da = jax.random.normal(ks[8], (NL, F, R), dtype=jnp.float32) * s
        Db = jax.random.normal(ks[9], (NL, R, D), dtype=jnp.float32) * s
        Wr = jax.random.normal(ks[10], (D, E), dtype=jnp.float32) * s
        temperature = jnp.ones((1,), dtype=jnp.float32)
        return {'x': x, 'Wg': Wg, 'Wu': Wu, 'Wd': Wd, 'Ga': Ga, 'Gb': Gb, 'Ua': Ua, 'Ub': Ub, 'Da': Da, 'Db': Db, 'Wr': Wr, 'temperature': temperature}
    _L0_ffn_all = _L0_ffn_setup()
    _L0_ffn_in = {k: v for k, v in _L0_ffn_all.items() if k in ('Wg', 'Wu', 'Wd', 'Ga', 'Gb', 'Ua', 'Ub', 'Da', 'Db', 'Wr', 'temperature')}
    del _L0_ffn_all
    return {'x': x, 'ctx_512': ctx_512, 'L0_xattn_W_k': _L0_xattn_in['W_k'], 'L0_xattn_b_k': _L0_xattn_in['b_k'], 'L0_xattn_ln_gamma': _L0_xattn_in['ln_gamma'], 'L0_xattn_ln_beta': _L0_xattn_in['ln_beta'], 'L0_ffn_Wg': _L0_ffn_in['Wg'], 'L0_ffn_Wu': _L0_ffn_in['Wu'], 'L0_ffn_Wd': _L0_ffn_in['Wd'], 'L0_ffn_Ga': _L0_ffn_in['Ga'], 'L0_ffn_Gb': _L0_ffn_in['Gb'], 'L0_ffn_Ua': _L0_ffn_in['Ua'], 'L0_ffn_Ub': _L0_ffn_in['Ub'], 'L0_ffn_Da': _L0_ffn_in['Da'], 'L0_ffn_Db': _L0_ffn_in['Db'], 'L0_ffn_Wr': _L0_ffn_in['Wr'], 'L0_ffn_temperature': _L0_ffn_in['temperature']}

def reference(x, ctx_512, L0_xattn_W_k, L0_xattn_b_k, L0_xattn_ln_gamma, L0_xattn_ln_beta, L0_ffn_Wg, L0_ffn_Wu, L0_ffn_Wd, L0_ffn_Ga, L0_ffn_Gb, L0_ffn_Ua, L0_ffn_Ub, L0_ffn_Da, L0_ffn_Db, L0_ffn_Wr, L0_ffn_temperature):
    import jax
    import jax.numpy as jnp

    def _L0_xattn_ref(p, k_v, W_k, b_k, ln_gamma, ln_beta):
        import jax, jax.numpy as jnp
        import numpy as np
        EPS = 1e-06
        IMAGE_DIMS = 512
        kv = k_v @ W_k.T + b_k
        out = jnp.einsum('bij,bjd->bid', p, kv)
        scale = IMAGE_DIMS ** (-0.5)
        sim = jnp.einsum('bid,bjd->bij', out, kv) * scale
        mu = jnp.mean(sim, axis=-1, keepdims=True)
        var = jnp.var(sim, axis=-1, keepdims=True)
        sim = (sim - mu) * jax.lax.rsqrt(var + EPS) * ln_gamma + ln_beta
        attn = jax.nn.softmax(sim, axis=-1)
        return attn

    def _L0_ffn_ref(x, Wg, Wu, Wd, Ga, Gb, Ua, Ub, Da, Db, Wr, temperature):
        import jax, jax.numpy as jnp
        import numpy as np
        import math
        GOLDEN_CENTER = 1.0 / math.e
        GOLDEN_LOWER = 0.5 - math.log(4.0 / 3.0)
        GOLDEN_UPPER = 0.5
        B, T, D = (4, 256, 512)
        E = 8
        F = 2048 // (E // 2)
        R = 64
        NL = 2

        def _router_weights(x, Wr, temperature):
            logits = jnp.einsum('btd,de->bte', x, Wr)
            inhibition = jax.nn.sigmoid(logits / temperature)
            in_zone = (inhibition >= GOLDEN_LOWER) & (inhibition <= GOLDEN_UPPER)
            distance = jnp.abs(inhibition - GOLDEN_CENTER)
            w = jnp.exp(-distance / 0.1) * in_zone.astype(x.dtype)
            wsum = w.sum(axis=-1, keepdims=True)
            no_expert = wsum < 1e-08
            fb = jnp.exp(-distance / 0.3)
            _, top2 = jax.lax.top_k(fb, 2)
            fb_mask = jax.nn.one_hot(top2, E, dtype=x.dtype).sum(axis=-2)
            fb_w = fb * fb_mask
            fb_w = fb_w / jnp.clip(fb_w.sum(axis=-1, keepdims=True), 1e-08)
            w = jnp.where(no_expert, fb_w, w)
            return w / jnp.clip(w.sum(axis=-1, keepdims=True), 1e-08)
        weights = _router_weights(x, Wr, temperature)
        gate = jnp.einsum('btd,edf->ebtf', x, Wg)
        up = jnp.einsum('btd,edf->ebtf', x, Wu)
        gate = gate.at[:NL].add(jnp.einsum('btd,edr,erf->ebtf', x, Ga, Gb))
        up = up.at[:NL].add(jnp.einsum('btd,edr,erf->ebtf', x, Ua, Ub))
        mid = jax.nn.silu(gate) * up
        out = jnp.einsum('ebtf,efd->ebtd', mid, Wd)
        out = out.at[:NL].add(jnp.einsum('ebtf,efr,erd->ebtd', mid[:NL], Da, Db))
        return jnp.einsum('bte,ebtd->btd', weights, out)
    x = x + _L0_xattn_ref(_layernorm(x, axis=-1), ctx_512, L0_xattn_W_k, L0_xattn_b_k, L0_xattn_ln_gamma, L0_xattn_ln_beta)
    x = x + _L0_ffn_ref(_layernorm(x, axis=-1), L0_ffn_Wg, L0_ffn_Wu, L0_ffn_Wd, L0_ffn_Ga, L0_ffn_Gb, L0_ffn_Ua, L0_ffn_Ub, L0_ffn_Da, L0_ffn_Db, L0_ffn_Wr, L0_ffn_temperature)
    return x

_drawn_inputs = setup_inputs


def setup_inputs(seed=0):
    import zlib

    import numpy as np

    out = dict(_drawn_inputs(seed))
    spreads = {'L0_xattn_b_k': (0.0, 0.8),
     'L0_xattn_ln_gamma': (1.0, 0.6),
     'L0_xattn_ln_beta': (0.0, 0.8)}
    factors = {'ctx_512': 8.0,
     'L0_xattn_W_k': 8.0,
     'L0_ffn_Ga': 8.0,
     'L0_ffn_Gb': 8.0,
     'L0_ffn_Ua': 8.0,
     'L0_ffn_Ub': 8.0,
     'L0_ffn_Da': 8.0,
     'L0_ffn_Db': 8.0}
    for name, (base, spread) in spreads.items():
        noise = np.random.default_rng([zlib.crc32(name.encode()), seed]).standard_normal(out[name].shape)
        drawn = base * np.exp(spread * noise) if base else spread * noise
        out[name] = jnp.asarray(drawn.astype(out[name].dtype))
    for name, factor in factors.items():
        out[name] = (out[name] * factor).astype(out[name].dtype)
    return out
```

```python
import math
from contextlib import ExitStack

import concourse.bass as bass
from concourse import mybir

B, S, D = 4, 512, 512
C = 128
E, F, R = 8, 512, 64
P = 128
KT = D // P
FT = F // P
TT = S // P
NBLK = B

FIRST_EXPERT, LAST_EXPERT = 0, 1
POSITIONS = E

UNIT_CREDIT = 2
BLOCK_CREDIT = 4

GOLDEN_CENTER = 1.0 / math.e
GOLDEN_LOWER = 0.5 - math.log(4.0 / 3.0)
Z_LOWER = math.log(GOLDEN_LOWER / (1.0 - GOLDEN_LOWER))
Z_UPPER = 2.0 ** -23
SCALE = 512.0 ** -0.5
LN_EPS = 1e-5
SIM_EPS = 1e-6

N_CONST = 7
ROUTER_STEPS = 22
PT_BANK = [3, 2, 0, 1]


def xattn_ffn_kernel(nc, x, ctxT, wkT, bk, gamma, beta, wg, wu, wd, loraT, lora, wr, temperature, out):
    fp32 = mybir.dt.float32
    f32r = mybir.dt.float32r
    ALU = mybir.AluOpType
    ACT = mybir.ActivationFunctionType
    AX = mybir.AxisListType

    with ExitStack() as ctx:
        def sb(name, shape, dt=fp32):
            return ctx.enter_context(nc.sbuf_tensor(name, shape, dt))

        def sem(name):
            return ctx.enter_context(nc.semaphore(name))

        xacc = sb("xacc", [P, B * TT * D])
        xT_hi = sb("xT_hi", [P, KT, B * S], f32r)
        xT_lo = sb("xT_lo", [P, KT, B * S], f32r)
        w_raw = sb("w_raw", [P, 3, 4, 512])
        w_hi = sb("w_hi", [P, 3, 4, 512], f32r)
        w_lo = sb("w_lo", [P, 3, 4, 512], f32r)
        mid_hi = sb("mid_hi", [P, FT, S], f32r)
        mid_lo = sb("mid_lo", [P, FT, S], f32r)
        silu = sb("silu", [P, 2, S])
        mid = sb("mid", [P, 2, S])
        zt = sb("zt", [P, TT, S])
        beta_sb = sb("beta_sb", [P, S])
        bk_col = sb("bk_col", [P, 1])
        wr_sb = sb("wr_sb", [P, KT, E])
        temp_sb = sb("temp_sb", [P, 1])
        inv_temp = sb("inv_temp", [P, 1])
        half_less_center = sb("half_less_center", [P, 1])
        neg_half = sb("neg_half", [P, TT])
        below = sb("below", [P, E, E], mybir.dt.bfloat16)
        bn = sb("bn", [P, TT, 6])
        mv1 = sb("mv1", [P, TT, 2])
        mv2 = sb("mv2", [P, TT, 2])
        mv3 = sb("mv3", [P, TT, 2])
        var = sb("var", [P, 3, TT])
        rstd = sb("rstd", [P, 3, TT])
        sim_rs = sb("sim_rs", [P, TT])
        negmax = sb("negmax", [P, TT])
        esum = sb("esum", [P, TT])
        rsum = sb("rsum", [P, TT])
        z = sb("z", [P, TT, E])
        dist = sb("dist", [P, TT, E])
        tanh_z = sb("tanh_z", [P, TT, E])
        w_zone = sb("w_zone", [P, TT, E])
        fb = sb("fb", [P, TT, E])
        zone = sb("zone", [P, TT, E])
        rank = sb("rank", [P, TT, E])
        beats = sb("beats", [P, TT, E, E], mybir.dt.uint8)
        ties = sb("ties", [P, TT, E, E], mybir.dt.uint8)
        rsums = sb("rsums", [P, 6, TT])
        rw = sb("rw", [P, B * TT * E])

        def in_raw(first, n):
            return w_raw[:, :, :, :].rearrange("p m k c -> p (m k c)")[:, first * 512:(first + n) * 512]
        pT = in_raw(0, 4).rearrange("p (k i) -> p k i", k=4)
        kv = in_raw(4, 1).rearrange("p (j d) -> p j d", j=4)
        kvT = in_raw(5, 1)
        ctxT_sb = in_raw(6, 1)
        outT = in_raw(7, 1)
        xn = in_raw(8, 2).rearrange("p (u c) -> p u c", u=2)

        bk_row = in_raw(10, 1)[:, 0:C]
        wkT_sb = in_raw(10, 1)[:, C:2 * C]
        ident = in_raw(10, 1)[:, 2 * C:2 * C + P]
        gamma_sb = in_raw(11, 1)

        tiles = ctx.enter_context(nc.psum_tensor("tiles", [P, 4, 512], fp32))
        gate_up = ctx.enter_context(nc.psum_tensor("gate_up", [P, 4, 512], fp32))

        const_loaded = sem("const_loaded")
        consts_made = sem("consts_made")
        masks_made = sem("masks_made")
        inv_temp_made = sem("inv_temp_made")
        x_loaded = sem("x_loaded")
        ctx_loaded = sem("ctx_loaded")
        gu_loaded = sem("gu_loaded")
        d_loaded = sem("d_loaded")
        lora_loaded = sem("lora_loaded")
        lora_mm = sem("lora_mm")
        lora_added = sem("lora_added")
        w_hi_made = sem("w_hi_made")
        w_gu_ready = sem("w_gu_ready")
        w_d_ready = sem("w_d_ready")
        bn_done = [sem(f"bn_done{i}") for i in range(3)]
        mv_done = [sem(f"mv_done{i}") for i in range(3)]
        eps_set = [sem(f"eps_set{i}") for i in range(3)]
        var_ready = [sem(f"var_ready{i}") for i in range(3)]
        rstd_ready = [sem(f"rstd_ready{i}") for i in range(3)]
        xn_ready = sem("xn_ready")
        transposed = sem("transposed")
        kv_mm = sem("kv_mm")
        kv_ready = sem("kv_ready")
        kvT_ready = sem("kvT_ready")
        pT_ready = sem("pT_ready")
        out_mm = sem("out_mm")
        outT_ready = sem("outT_ready")
        sim_mm = sem("sim_mm")
        sim_rs_ready = sem("sim_rs_ready")
        sim_read = sem("sim_read")
        z_ready = sem("z_ready")
        max_ready = sem("max_ready")
        exp_done = sem("exp_done")
        rsum_ready = sem("rsum_ready")
        x2_ready = sem("x2_ready")
        x2nT_ready = sem("x2nT_ready")
        xT_hi_ready = sem("xT_hi_ready")
        xT_lo_ready = sem("xT_lo_ready")
        logits_mm = sem("logits_mm")
        logits_read = sem("logits_read")
        router_act = sem("router_act")
        router_dve = sem("router_dve")
        rw_ready = sem("rw_ready")
        gu_mm = sem("gu_mm")
        silu_made = sem("silu_made")
        mid_made = sem("mid_made")
        hi_made = sem("hi_made")
        lo_made = sem("lo_made")
        down_mm = sem("down_mm")
        acc_done = sem("acc_done")
        stored = sem("stored")

        def reach(eng, s, count):
            if not isinstance(count, int) or count > 0:
                eng.wait_ge(s, count)

        def tile_of(a, t):
            return xacc[:, bass.ds((a * TT + t) * D, D)]

        def plain(ap):
            return ap.bitcast(fp32)

        def first_raw(m):
            return xacc[:, (1 + m) * TT * D:(2 + m) * TT * D].rearrange("p (k c) -> p k c", k=4)

        LORA_PARTS = [(0, 0), (64, 0), (0, 2)]

        def lora_slot(r, slot):
            if r:
                return zt[:, slot, :]
            return mid[:, slot, :] if slot < 2 else silu[:, slot - 2, :]

        block = ctx.enter_context(nc.Block())

        @block.sync
        def _(sp):
            def load_x(a):
                sp.dma_start(xacc[:, a * TT * D:(a + 1) * TT * D].rearrange("p (t c) -> p t c", t=TT),
                             x[a, :, :].rearrange("(t p) c -> p t c", p=P)).then_inc(x_loaded, 16)

            def load_gate_up(e):
                for m, w in enumerate((wg, wu)):
                    sp.dma_start(w_raw[:, m, :, :], w[bass.ds(e, 1), :, :].rearrange("o (k p) f -> p (o k) f", p=P))\
                      .then_inc(gu_loaded, 16)

            def load_down(e):
                sp.dma_start(w_raw[:, 2, :, :], wd[bass.ds(e, 1), :, :].rearrange("o (k p) f -> p (o k) f", p=P))\
                  .then_inc(d_loaded, 16)

            def load_lora(r, e):
                for m, (p0, slot) in enumerate(LORA_PARTS):
                    sp.dma_start(lora_slot(r, slot)[p0:p0 + R, :], loraT[m, e, :, :]).then_inc(lora_loaded, 16)
                    sp.dma_start(lora_slot(r, slot + 1)[p0:p0 + R, :], lora[m, e, :, :]).then_inc(lora_loaded, 16)

            load_x(0)
            sp.dma_start(ctxT_sb, ctxT[0, :, :]).then_inc(ctx_loaded, 16)
            load_lora(0, FIRST_EXPERT)
            for m, w in enumerate((wg, wu)):
                sp.dma_start(first_raw(m), w[FIRST_EXPERT, :, :].rearrange("(k p) f -> p k f", p=P)).then_inc(gu_loaded, 16)
            sp.dma_start(first_raw(2), wd[FIRST_EXPERT, :, :].rearrange("(k p) f -> p k f", p=P)).then_inc(d_loaded, 16)
            for a in range(1, B):
                sp.wait_ge(w_gu_ready, 4)
                if a == 3:
                    sp.wait_ge(w_d_ready, 1)
                sp.wait_ge(x_loaded, 16 * a)
                load_x(a)
                if a > 1:
                    sp.wait_ge(ctx_loaded, 16 * a)
                sp.wait_ge(kv_mm, a)
                sp.dma_start(ctxT_sb, ctxT[a, :, :]).then_inc(ctx_loaded, 16)

            sp.wait_ge(xT_lo_ready, B * TT)
            sp.wait_ge(transposed, 8 * B)
            sp.wait_ge(logits_mm, B)
            load_gate_up(2)
            load_down(2)
            sp.wait_ge(x2_ready, B * TT)
            load_lora(1, LAST_EXPERT)
            with sp.Fori(2, POSITIONS - 1) as s:
                sp.wait_ge(w_gu_ready, s * 4)
                load_gate_up(s + 1)
                sp.wait_ge(w_d_ready, s)
                load_down(s + 1)
            sp.wait_ge(w_gu_ready, (POSITIONS - 1) * 4)
            load_gate_up(LAST_EXPERT)
            sp.wait_ge(w_d_ready, POSITIONS - 1)
            load_down(LAST_EXPERT)

            for i in range(B * TT):
                sp.wait_ge(acc_done, BLOCK_CREDIT + (POSITIONS - 1) * B * TT + i + 1)
                sp.dma_start(out[i // TT, (i % TT) * P:(i % TT + 1) * P, :], xacc[:, i * D:(i + 1) * D])\
                  .then_inc(stored, 16)
            sp.wait_ge(stored, 16 * B * TT)

        @block.gpsimd
        def _(pool):
            nc.gpsimd.memset(ident[:, :], 0.0).then_inc(consts_made, 1)
            nc.gpsimd.memset(below[:, :, :], 1.0).then_inc(consts_made, 1)
            nc.gpsimd.memset(neg_half[:, :], -0.5).then_inc(consts_made, 1)
            pool.wait_ge(consts_made, 3)
            nc.gpsimd.affine_select(out=ident[:, :], in_=ident[:, :], compare_op=ALU.not_equal, fill=1.0,
                                    base=0, pattern=[[-1, P]], channel_multiplier=1).then_inc(masks_made, 1)
            nc.gpsimd.affine_select(out=below[:, :, :], in_=below[:, :, :], compare_op=ALU.is_gt, fill=0.0,
                                    base=0, pattern=[[1, E], [-1, E]], channel_multiplier=0).then_inc(masks_made, 1)
            pool.sem_inc(lo_made, UNIT_CREDIT)

            def inverse_root(a, i):
                pool.wait_ge(var_ready[i], a + 1)
                nc.gpsimd.tensor_tensor(rstd[:, i, :], var[:, i, :], neg_half[:, :], ALU.pow)\
                  .then_inc(rstd_ready[i], 1)

            def low_part(n, f):
                pool.wait_ge(hi_made, n * FT + f + 1)
                pool.wait_ge(down_mm, n * TT + BLOCK_CREDIT)
                nc.gpsimd.tensor_tensor(mid_lo[:, f, :], mid[:, f % 2, :], plain(mid_hi[:, f, :]), ALU.subtract)\
                  .then_inc(lo_made, 1)

            def x_low_parts(a):
                for t in range(TT):
                    pool.wait_ge(xT_hi_ready, a * TT + t + 1)
                    cols = bass.ds(a * S + t * P, P)
                    nc.gpsimd.tensor_tensor(xT_lo[:, :, cols], pT[:, :, t * P:(t + 1) * P],
                                            plain(xT_hi[:, :, cols]), ALU.subtract).then_inc(xT_lo_ready, 1)

            def first_low_parts():
                for f in range(FT):
                    cols = slice(f * P, (f + 1) * P)
                    pool.wait_ge(w_hi_made, f + 1)
                    for m in range(2):
                        ins = nc.gpsimd.tensor_tensor(w_lo[:, m, :, cols], first_raw(m)[:, :, cols],
                                                      plain(w_hi[:, m, :, cols]), ALU.subtract)
                    ins.then_inc(w_gu_ready, 1)
                pool.wait_ge(w_hi_made, 5)
                nc.gpsimd.tensor_tensor(w_lo[:, 2, :, :], first_raw(2), plain(w_hi[:, 2, :, :]), ALU.subtract)\
                  .then_inc(w_d_ready, 1)

            for i in range(3):
                inverse_root(0, i)
            first_low_parts()
            x_low_parts(0)
            with pool.Fori(0, B - 1) as n:
                inverse_root(n + 1, 0)
                low_part(n, 0)
                low_part(n, 1)
                inverse_root(n + 1, 1)
                low_part(n, 2)
                low_part(n, 3)
                inverse_root(n + 1, 2)
                x_low_parts(n + 1)
            with pool.Fori(B - 1, POSITIONS * NBLK) as n:
                for f in range(FT):
                    low_part(n, f)

        @block.scalar
        def _(act):
            act.dma_start(wkT_sb, wkT).then_inc(const_loaded, 16)
            act.dma_start(bk_col[:, :], bk.rearrange("(d o) -> d o", o=1)).then_inc(const_loaded, 16)
            act.dma_start(bk_row, bk.partition_broadcast(P)).then_inc(const_loaded, 16)
            act.dma_start(gamma_sb[:, :], gamma.partition_broadcast(P)).then_inc(const_loaded, 16)
            act.dma_start(beta_sb[:, :], beta.partition_broadcast(P)).then_inc(const_loaded, 16)
            act.dma_start(wr_sb[:, :, :], wr.rearrange("(k p) e -> p k e", p=P)).then_inc(const_loaded, 16)
            act.dma_start(temp_sb[:, :], temperature.partition_broadcast(P)).then_inc(const_loaded, 16)

            def split_gate_up(g, f, src):
                cols = slice(f * P, (f + 1) * P)
                for m in range(2):
                    ins = nc.scalar.activation(w_hi[:, m, :, cols], src(m)[:, :, cols], ACT.Copy)
                ins.then_inc(w_hi_made, 1)

            def split_down(src):
                nc.scalar.activation(w_hi[:, 2, :, :], src(2), ACT.Copy).then_inc(w_hi_made, 1)

            def raw(m):
                return w_raw[:, m, :, :]

            def unit(n, f):
                act.wait_ge(gu_mm, n * FT + f + 1)
                act.wait_ge(mid_made, n * FT + f - 1 + UNIT_CREDIT)
                nc.scalar.activation(silu[:, f % 2, :], gate_up[:, 2 * (f % 2), :], ACT.Silu).then_inc(silu_made, 1)
                act.wait_ge(mid_made, n * FT + f + 1 + UNIT_CREDIT)
                act.wait_ge(down_mm, n * TT + BLOCK_CREDIT)
                nc.scalar.activation(mid_hi[:, f, :], mid[:, f % 2, :], ACT.Copy).then_inc(hi_made, 1)

            def kvT_bias(a):
                act.wait_ge(kv_mm, a + 1)
                nc.scalar.activation(kvT, tiles[:, 1, :], ACT.Identity, bias=bk_col[:, 0:1]).then_inc(kvT_ready, 1)

            def copy_pT(a):
                for t in range(TT):
                    act.wait_ge(transposed, 8 * a + t + 1)
                    if t == 0:
                        reach(act, xT_lo_ready, a * TT)
                    nc.scalar.activation(pT[:, :, t * P:(t + 1) * P],
                                         tiles[:, PT_BANK[t], :].rearrange("p (k i) -> p k i", k=KT), ACT.Copy)\
                      .then_inc(pT_ready, 1)

            def copy_outT(a):
                act.wait_ge(out_mm, a + 1)
                nc.scalar.activation(outT, tiles[:, 0, :], ACT.Copy).then_inc(outT_ready, 1)

            def router_functions(a):
                act.wait_ge(logits_read, a + 1)
                nc.scalar.activation(tanh_z[:, :, :], z[:, :, :], ACT.Tanh, scale=0.5).then_inc(router_act, 1)
                act.wait_ge(router_act, 4 * a + 1)
                nc.scalar.activation(dist[:, :, :], tanh_z[:, :, :], ACT.Abs, scale=0.5, bias=half_less_center[:, 0:1])\
                  .then_inc(router_act, 1)
                act.wait_ge(router_act, 4 * a + 2)
                nc.scalar.activation(w_zone[:, :, :], dist[:, :, :], ACT.Exp, scale=-1.0 / 0.1).then_inc(router_act, 1)
                nc.scalar.activation(fb[:, :, :], dist[:, :, :], ACT.Exp, scale=-1.0 / 0.3).then_inc(router_act, 1)

            def exps(a):
                for t in range(TT):
                    act.wait_ge(max_ready, a * TT + t + 1)
                    nc.scalar.activation(zt[:, t, :], zt[:, t, :], ACT.Exp, bias=negmax[:, t:t + 1],
                                         accum_out=esum[:, t:t + 1]).then_inc(exp_done, 1)

            def copy_x2nT(a):
                for t in range(TT):
                    act.wait_ge(transposed, 8 * a + 4 + t + 1)
                    nc.scalar.activation(pT[:, :, t * P:(t + 1) * P],
                                         gate_up[:, t, :].rearrange("p (k i) -> p k i", k=KT), ACT.Copy)\
                      .then_inc(x2nT_ready, 1)
                    act.wait_ge(x2nT_ready, a * TT + t + 1)
                    nc.scalar.activation(xT_hi[:, :, bass.ds(a * S + t * P, P)], pT[:, :, t * P:(t + 1) * P], ACT.Copy)\
                      .then_inc(xT_hi_ready, 1)

            act.wait_ge(const_loaded, 16 * N_CONST)
            kvT_bias(0)
            copy_pT(0)
            copy_outT(0)
            exps(0)
            act.wait_ge(lora_added, 12)
            for f in range(FT):
                split_gate_up(0, f, first_raw)
            split_down(first_raw)
            copy_x2nT(0)
            with act.Fori(0, B - 1) as n:
                unit(n, 0)
                kvT_bias(n + 1)
                copy_pT(n + 1)
                unit(n, 1)
                router_functions(n)
                copy_outT(n + 1)
                unit(n, 2)
                unit(n, 3)
                exps(n + 1)
                copy_x2nT(n + 1)
            unit(B - 1, 0)
            unit(B - 1, 1)
            router_functions(B - 1)
            unit(B - 1, 2)
            act.wait_ge(gu_loaded, 64)
            for f in range(FT - 1):
                split_gate_up(1, f, raw)
            unit(B - 1, 3)
            split_gate_up(1, FT - 1, raw)
            act.wait_ge(down_mm, NBLK * TT + BLOCK_CREDIT)
            act.wait_ge(d_loaded, 32)
            split_down(raw)

            def expert(s, lora_count=0):
                with act.Fori(0, B - 1) as b:
                    for f in range(FT):
                        unit(s * NBLK + b, f)
                n = s * NBLK + B - 1
                for f in range(FT):
                    unit(n, f)
                    if f == 0:
                        act.wait_ge(gu_loaded, (s + 2) * 32)
                        reach(act, lora_added, lora_count)
                    split_gate_up(s + 1, f, raw)
                act.wait_ge(down_mm, (n + 1) * TT + BLOCK_CREDIT)
                act.wait_ge(d_loaded, (s + 2) * 16)
                split_down(raw)

            with act.Fori(1, POSITIONS - 2) as s:
                expert(s)
            expert(POSITIONS - 2, lora_count=24)
            with act.Fori((POSITIONS - 1) * NBLK, POSITIONS * NBLK) as n:
                for f in range(FT):
                    unit(n, f)

        @block.vector
        def _(dve):
            dve.sem_inc(mid_made, UNIT_CREDIT)
            dve.sem_inc(acc_done, BLOCK_CREDIT)
            nc.vector.memset(half_less_center[:, :], 0.5 - GOLDEN_CENTER).then_inc(inv_temp_made, 1)
            dve.wait_ge(const_loaded, 16 * N_CONST)
            nc.vector.reciprocal(inv_temp[:, :], temp_sb[:, :]).then_inc(inv_temp_made, 1)

            def set_eps(i, half, eps):
                nc.vector.memset(var[:, i, 2 * half:2 * half + 2], eps).then_inc(eps_set[i], 1)

            def spread(i, mv, a, scale, eps):
                dve.wait_ge(bn_done[i], (a + 1) * TT)
                set_eps(i, 1, eps)
                for t in range(TT):
                    nc.vector.bn_aggr(mv[:, t, :], bn[:, t, :]).then_inc(mv_done[i], 1)
                dve.wait_ge(eps_set[i], 2 * a + 2)
                dve.wait_ge(mv_done[i], (a + 1) * TT)
                nc.vector.scalar_tensor_tensor(var[:, i, :], mv[:, :, 1], scale, var[:, i, :], ALU.mult, ALU.add)\
                  .then_inc(var_ready[i], 1)

            def normalise(i, mv, a, t, half):
                reach(dve, transposed, 8 * a + 4 * half + t - 1)
                nc.vector.tensor_scalar(xn[:, t % 2, :], tile_of(a, t), mv[:, t, 0:1], rstd[:, i, t:t + 1],
                                        ALU.subtract, ALU.mult).then_inc(xn_ready, 1)

            def ln1_stats(a):
                dve.wait_ge(x_loaded, 16 * a + 16)
                set_eps(0, 0, LN_EPS)
                for t in range(TT):
                    nc.vector.bn_stats(bn[:, t, :], tile_of(a, t)).then_inc(bn_done[0], 1)
                spread(0, mv1, a, 1.0, LN_EPS)
                dve.wait_ge(rstd_ready[0], a + 1)

            def kv_bias(a):
                dve.wait_ge(kv_mm, a + 1)
                nc.vector.tensor_tensor(kv, tiles[:, 0, :].rearrange("p (j d) -> p j d", j=4),
                                        bk_row[:, None, :].broadcast_to([P, 4, C]), ALU.add).then_inc(kv_ready, 1)

            def sim_scores(a):
                for t in range(TT):
                    dve.wait_ge(sim_mm, a * TT + t + 1)
                    if t == 0:
                        set_eps(1, 0, SIM_EPS)
                    nc.vector.bn_stats(bn[:, t, :], tiles[:, t, :]).then_inc(bn_done[1], 1)
                spread(1, mv2, a, SCALE * SCALE, SIM_EPS)
                for t in range(TT):
                    nc.vector.scalar_tensor_tensor(zt[:, t, :], tiles[:, t, :], mv2[:, t, 0:1], gamma_sb[:, :],
                                                   ALU.subtract, ALU.mult).then_inc(sim_read, 1)
                dve.wait_ge(rstd_ready[1], a + 1)
                nc.vector.tensor_scalar(sim_rs[:, :], rstd[:, 1, :], SCALE, None, ALU.mult).then_inc(sim_rs_ready, 1)

            def sim_norm(a):
                dve.wait_ge(sim_rs_ready, a + 1)
                for t in range(TT):
                    dve.wait_ge(sim_read, a * TT + t + 1)
                    nc.vector.scalar_tensor_tensor(zt[:, t, :], zt[:, t, :], sim_rs[:, t:t + 1], beta_sb[:, :],
                                                   ALU.mult, ALU.add).then_inc(z_ready, 1)
                for t in range(TT):
                    dve.wait_ge(z_ready, a * TT + t + 1)
                    nc.vector.tensor_reduce(negmax[:, t:t + 1], zt[:, t, :], AX.X, ALU.max, negate=True)\
                      .then_inc(max_ready, 1)

            def add_attention(a):
                for t in range(TT):
                    dve.wait_ge(exp_done, a * TT + t + 1)
                    nc.vector.reciprocal(rsum[:, t:t + 1], esum[:, t:t + 1]).then_inc(rsum_ready, 1)
                    dve.wait_ge(rsum_ready, a * TT + t + 1)
                    nc.vector.scalar_tensor_tensor(tile_of(a, t), zt[:, t, :], rsum[:, t:t + 1], tile_of(a, t),
                                                   ALU.mult, ALU.add).then_inc(x2_ready, 1)
                dve.wait_ge(x2_ready, a * TT + TT)
                set_eps(2, 0, LN_EPS)
                for t in range(TT):
                    nc.vector.bn_stats(bn[:, t, :], tile_of(a, t)).then_inc(bn_done[2], 1)
                spread(2, mv3, a, 1.0, LN_EPS)
                dve.wait_ge(rstd_ready[2], a + 1)

            def read_logits(a):
                dve.wait_ge(logits_mm, a + 1)
                nc.vector.tensor_scalar(z[:, :, :], tiles[:, 2, 0:TT * E].rearrange("p (t e) -> p t e", t=TT),
                                        inv_temp[:, 0:1], None, ALU.mult).then_inc(logits_read, 1)

            def router(a):
                count = [0]

                def step(ins):
                    ins.then_inc(router_dve, 1)
                    count[0] += 1
                    dve.wait_ge(router_dve, a * ROUTER_STEPS + count[0])

                def over_experts(v):
                    return v[:, :, None].broadcast_to([P, TT, E])

                dve.wait_ge(logits_read, a + 1)
                step(nc.vector.tensor_scalar(zone[:, :, :], z[:, :, :], Z_LOWER, None, ALU.is_ge))
                step(nc.vector.scalar_tensor_tensor(zone[:, :, :], z[:, :, :], Z_UPPER, zone[:, :, :],
                                                    ALU.is_le, ALU.mult))
                dve.wait_ge(router_act, 4 * a + 4)
                step(nc.vector.tensor_tensor(w_zone[:, :, :], w_zone[:, :, :], zone[:, :, :], ALU.mult))
                step(nc.vector.tensor_reduce(rsums[:, 0, :], w_zone[:, :, :], AX.X, ALU.add))
                step(nc.vector.tensor_scalar(rsums[:, 1, :], rsums[:, 0, :], 1e-8, None, ALU.is_lt))
                mine = fb[:, :, :, None].broadcast_to([P, TT, E, E])
                other = fb[:, :, None, :].broadcast_to([P, TT, E, E])
                step(nc.vector.tensor_tensor(beats[:, :, :, :], other, mine, ALU.is_gt))
                step(nc.vector.tensor_tensor(ties[:, :, :, :], other, mine, ALU.is_equal))
                step(nc.vector.tensor_tensor(ties[:, :, :, :], ties[:, :, :, :],
                                             below[:, None, :, :].broadcast_to([P, TT, E, E]), ALU.mult))
                step(nc.vector.tensor_tensor(beats[:, :, :, :], beats[:, :, :, :], ties[:, :, :, :], ALU.add))
                step(nc.vector.tensor_reduce(rank[:, :, :], beats[:, :, :, :], AX.X, ALU.add))
                step(nc.vector.scalar_tensor_tensor(fb[:, :, :], rank[:, :, :], 2.0, fb[:, :, :], ALU.is_lt, ALU.mult))
                step(nc.vector.tensor_reduce(rsums[:, 2, :], fb[:, :, :], AX.X, ALU.add))
                step(nc.vector.tensor_scalar(rsums[:, 2, :], rsums[:, 2, :], 1e-8, None, ALU.max))
                step(nc.vector.reciprocal(rsums[:, 3, :], rsums[:, 2, :]))
                step(nc.vector.tensor_tensor(rsums[:, 3, :], rsums[:, 3, :], rsums[:, 1, :], ALU.mult))
                step(nc.vector.tensor_tensor(fb[:, :, :], fb[:, :, :], over_experts(rsums[:, 3, :]), ALU.mult))
                step(nc.vector.tensor_scalar(rsums[:, 4, :], rsums[:, 0, :], 1e-8, None, ALU.is_ge))
                step(nc.vector.tensor_tensor(w_zone[:, :, :], w_zone[:, :, :], over_experts(rsums[:, 4, :]), ALU.mult))
                step(nc.vector.tensor_tensor(w_zone[:, :, :], w_zone[:, :, :], fb[:, :, :], ALU.add))
                step(nc.vector.tensor_reduce(rsums[:, 5, :], w_zone[:, :, :], AX.X, ALU.add))
                step(nc.vector.tensor_scalar(rsums[:, 5, :], rsums[:, 5, :], 1e-8, None, ALU.max))
                step(nc.vector.reciprocal(rsums[:, 5, :], rsums[:, 5, :]))
                assert count[0] == ROUTER_STEPS
                nc.vector.tensor_tensor(rw[:, bass.ds(a * TT * E, TT * E)].rearrange("p (t e) -> p t e", t=TT),
                                        w_zone[:, :, :], over_experts(rsums[:, 5, :]), ALU.mult).then_inc(rw_ready, 1)

            def unit(n, f):
                dve.wait_ge(silu_made, n * FT + f + 1)
                dve.wait_ge(lo_made, n * FT + f - 1 + UNIT_CREDIT)
                nc.vector.tensor_tensor(mid[:, f % 2, :], silu[:, f % 2, :], gate_up[:, 2 * (f % 2) + 1, :], ALU.mult)\
                  .then_inc(mid_made, 1)

            def accumulate(n, b, e):
                for t in range(TT):
                    dve.wait_ge(down_mm, n * TT + t + 1 + BLOCK_CREDIT)
                    nc.vector.scalar_tensor_tensor(tile_of(b, t), tiles[:, t, :],
                                                   rw[:, bass.ds((b * TT + t) * E + e, 1)], tile_of(b, t),
                                                   ALU.mult, ALU.add).then_inc(acc_done, 1)

            def split_gate_up(g, f, src):
                cols = slice(f * P, (f + 1) * P)
                dve.wait_ge(w_hi_made, g * 5 + f + 1)
                for m in range(2):
                    ins = nc.vector.tensor_tensor(w_lo[:, m, :, cols], src(m)[:, :, cols], plain(w_hi[:, m, :, cols]),
                                                  ALU.subtract)
                ins.then_inc(w_gu_ready, 1)

            def split_down(g, src):
                dve.wait_ge(w_hi_made, g * 5 + 5)
                nc.vector.tensor_tensor(w_lo[:, 2, :, :], src(2), plain(w_hi[:, 2, :, :]), ALU.subtract)\
                  .then_inc(w_d_ready, 1)

            def raw(m):
                return w_raw[:, m, :, :]

            def add_lora(r, banks, dst, m):
                for k in range(4):
                    dve.wait_ge(lora_mm, r * 12 + m * 4 + k + 1)
                    nc.vector.tensor_tensor(dst(m)[:, k, :], dst(m)[:, k, :], banks[:, k, :], ALU.add)\
                      .then_inc(lora_added, 1)

            ln1_stats(0)
            for t in range(2):
                normalise(0, mv1, 0, t, 0)
            kv_bias(0)
            for t in range(2, TT):
                normalise(0, mv1, 0, t, 0)
            sim_scores(0)
            sim_norm(0)
            dve.wait_ge(gu_loaded, 32)
            add_lora(0, gate_up, first_raw, 0)
            add_lora(0, gate_up, first_raw, 1)
            dve.wait_ge(d_loaded, 16)
            add_lora(0, gate_up, first_raw, 2)
            add_attention(0)
            for t in range(TT):
                normalise(2, mv3, 0, t, 1)
            with dve.Fori(0, B - 1) as n:
                a = n + 1
                ln1_stats(a)
                normalise(0, mv1, a, 0, 0)
                normalise(0, mv1, a, 1, 0)
                unit(n, 0)
                read_logits(n)
                kv_bias(a)
                normalise(0, mv1, a, 2, 0)
                normalise(0, mv1, a, 3, 0)
                unit(n, 1)
                router(n)
                sim_scores(a)
                unit(n, 2)
                sim_norm(a)
                unit(n, 3)
                add_attention(a)
                normalise(2, mv3, a, 0, 1)
                normalise(2, mv3, a, 1, 1)
                normalise(2, mv3, a, 2, 1)
                normalise(2, mv3, a, 3, 1)
                dve.wait_ge(rw_ready, n + 1)
                accumulate(n, n, FIRST_EXPERT)
            unit(B - 1, 0)
            read_logits(B - 1)
            unit(B - 1, 1)
            router(B - 1)
            unit(B - 1, 2)
            for f in range(FT - 1):
                split_gate_up(1, f, raw)
            unit(B - 1, 3)
            split_gate_up(1, FT - 1, raw)
            dve.wait_ge(rw_ready, B)
            accumulate(B - 1, B - 1, FIRST_EXPERT)
            split_down(1, raw)

            def expert(s, e, with_lora=False):
                with dve.Fori(0, B - 1) as b:
                    for f in range(FT):
                        unit(s * NBLK + b, f)
                    accumulate(s * NBLK + b, b, e)
                n = s * NBLK + B - 1
                if with_lora:
                    dve.wait_ge(gu_loaded, POSITIONS * 32)
                    dve.wait_ge(d_loaded, POSITIONS * 16)
                    for m in range(3):
                        add_lora(1, tiles, raw, m)
                for f in range(FT):
                    unit(n, f)
                    split_gate_up(s + 1, f, raw)
                accumulate(n, B - 1, e)
                split_down(s + 1, raw)

            with dve.Fori(1, POSITIONS - 2) as s:
                expert(s, s + 1)
            expert(POSITIONS - 2, POSITIONS - 1, with_lora=True)
            with dve.Fori(0, B) as b:
                for f in range(FT):
                    unit((POSITIONS - 1) * NBLK + b, f)
                accumulate((POSITIONS - 1) * NBLK + b, b, LAST_EXPERT)

        @block.tensor
        def _(pe):
            pe.sem_inc(down_mm, BLOCK_CREDIT)

            def three_passes(dst, w_h, w_l, x_h, x_l, first, last):
                nc.tensor.matmul(dst, w_h, x_h, start=first, stop=False)
                nc.tensor.matmul(dst, w_h, x_l, start=False, stop=False)
                return nc.tensor.matmul(dst, w_l, x_h, start=False, stop=last)

            def project_context(a):
                pe.wait_ge(ctx_loaded, 16 * a + 16)
                reach(pe, sim_read, a * TT)
                reach(pe, acc_done, a * TT)
                for j in range(4):
                    nc.tensor.matmul(tiles[:, 0, j * C:(j + 1) * C], ctxT_sb[:, j * P:(j + 1) * P], wkT_sb,
                                     start=True, stop=True)
                nc.tensor.matmul(tiles[:, 1, :], wkT_sb, ctxT_sb, start=True, stop=True).then_inc(kv_mm, 1)

            def transpose_tile(dst, src):
                for k in range(KT):
                    ins = nc.tensor.transpose(dst[:, k * P:(k + 1) * P], src[:, k * P:(k + 1) * P], ident[:, :])
                ins.then_inc(transposed, 1)

            def transpose_x(a):
                for t in range(TT):
                    pe.wait_ge(xn_ready, 8 * a + t + 1)
                    if t == 1:
                        reach(pe, logits_read, a)
                    if t == 2:
                        pe.wait_ge(kv_ready, a + 1)
                    if t == 3:
                        pe.wait_ge(kvT_ready, a + 1)
                    transpose_tile(tiles[:, PT_BANK[t], :], xn[:, t % 2, :])

            def attend(a):
                pe.wait_ge(pT_ready, a * TT + TT)
                for j in range(4):
                    ins = nc.tensor.matmul(tiles[:, 0, :], kv[:, j, :], pT[:, j, :], start=(j == 0), stop=(j == 3))
                ins.then_inc(out_mm, 1)
                pe.wait_ge(outT_ready, a + 1)
                for t in range(TT):
                    nc.tensor.matmul(tiles[:, t, :], outT[:, t * P:(t + 1) * P], kvT, start=True, stop=True)\
                      .then_inc(sim_mm, 1)

            def transpose_x2(a):
                reach(pe, mid_made, a * FT + UNIT_CREDIT)
                for t in range(TT):
                    pe.wait_ge(xn_ready, 8 * a + 4 + t + 1)
                    transpose_tile(gate_up[:, t, :], xn[:, t % 2, :])

            def route(a):
                pe.wait_ge(x2nT_ready, a * TT + TT)
                pe.wait_ge(acc_done, a * TT + BLOCK_CREDIT)
                for t in range(TT):
                    for k in range(KT):
                        ins = nc.tensor.matmul(tiles[:, 2, t * E:(t + 1) * E], pT[:, k, t * P:(t + 1) * P], wr_sb[:, k, :],
                                               start=(k == 0), stop=(k == KT - 1))
                ins.then_inc(logits_mm, 1)

            def unit(n, b, f):
                pe.wait_ge(mid_made, n * FT + f - 1 + UNIT_CREDIT)
                p = f % 2
                for m in range(2):
                    for k in range(KT):
                        cols = slice(f * P, (f + 1) * P)
                        tok = bass.ds(b * S, S)
                        ins = three_passes(gate_up[:, 2 * p + m, :], w_hi[:, m, k, cols], w_lo[:, m, k, cols],
                                           xT_hi[:, k, tok], xT_lo[:, k, tok], k == 0, k == KT - 1)
                ins.then_inc(gu_mm, 1)

            def down(n, f):
                pe.wait_ge(lo_made, n * FT + f + 1 + UNIT_CREDIT)
                for t in range(TT):
                    if f == 0:
                        pe.wait_ge(acc_done, n * TT + t + 1)
                    toks = slice(t * P, (t + 1) * P)
                    ins = three_passes(tiles[:, t, :], mid_hi[:, f, toks], mid_lo[:, f, toks],
                                       w_hi[:, 2, f, :], w_lo[:, 2, f, :], f == 0, f == FT - 1)
                    if f == FT - 1:
                        ins.then_inc(down_mm, 1)

            def low_rank(r, banks):
                pe.wait_ge(lora_loaded, 96 * (r + 1))
                for m, (p0, slot) in enumerate(LORA_PARTS):
                    for k in range(4):
                        if m:
                            pe.wait_ge(lora_added, r * 12 + (m - 1) * 4 + k + 1)
                        nc.tensor.matmul(banks[:, k, :], lora_slot(r, slot)[p0:p0 + R, k * P:(k + 1) * P],
                                         lora_slot(r, slot + 1)[p0:p0 + R, :], start=True, stop=True).then_inc(lora_mm, 1)

            pe.wait_ge(const_loaded, 16 * N_CONST)
            pe.wait_ge(masks_made, 2)
            project_context(0)
            transpose_x(0)
            attend(0)
            low_rank(0, gate_up)
            pe.wait_ge(lora_added, 12)
            transpose_x2(0)
            pe.wait_ge(w_gu_ready, 4)
            with pe.Fori(0, B - 1) as n:
                a = n + 1
                pe.wait_ge(xT_lo_ready, n * TT + TT)
                unit(n, n, 0)
                route(n)
                project_context(a)
                transpose_x(a)
                unit(n, n, 1)
                attend(a)
                unit(n, n, 2)
                unit(n, n, 3)
                pe.wait_ge(w_d_ready, 1)
                pe.wait_ge(sim_read, a * TT + TT)
                for f in range(FT - 1):
                    down(n, f)
                down(n, FT - 1)
                transpose_x2(a)
            pe.wait_ge(xT_lo_ready, B * TT)
            unit(B - 1, B - 1, 0)
            route(B - 1)
            for f in range(1, FT):
                unit(B - 1, B - 1, f)
            pe.wait_ge(logits_read, B)
            for f in range(FT):
                down(B - 1, f)

            def blocks(s, first, end):
                with pe.Fori(first, end) as b:
                    n = s * NBLK + b
                    for f in range(FT):
                        pe.wait_ge(w_gu_ready, s * 4 + f + 1)
                        unit(n, b, f)
                    pe.wait_ge(w_d_ready, s + 1)
                    for f in range(FT):
                        down(n, f)

            with pe.Fori(1, POSITIONS - 2) as s:
                blocks(s, 0, B)
            blocks(POSITIONS - 2, 0, B - 1)
            pe.wait_ge(acc_done, ((POSITIONS - 2) * NBLK + B - 1) * TT + BLOCK_CREDIT)
            low_rank(1, tiles)
            pe.wait_ge(lora_added, 24)
            blocks(POSITIONS - 2, B - 1, B)
            blocks(POSITIONS - 1, 0, B)


def kernel(**inputs):
    import numpy as _np
    import concourse.bacc as _bacc
    from concourse import mybir as _mybir
    from concourse.bass_utils import run_bass_kernel_spmd as _run

    def ffn(name):
        return _np.asarray(inputs["L0_ffn_" + name])

    given = {
        "x": inputs["x"],
        "ctxT": _np.asarray(inputs["ctx_512"]).transpose(0, 2, 1),
        "wkT": _np.asarray(inputs["L0_xattn_W_k"]).T,
        "bk": inputs["L0_xattn_b_k"],
        "gamma": inputs["L0_xattn_ln_gamma"],
        "beta": inputs["L0_xattn_ln_beta"],
        "wg": ffn("Wg"), "wu": ffn("Wu"), "wd": ffn("Wd"),
        "loraT": _np.stack([ffn(n).transpose(0, 2, 1) for n in ("Ga", "Ua", "Da")]),
        "lora": _np.stack([ffn(n) for n in ("Gb", "Ub", "Db")]),
        "wr": ffn("Wr"),
        "temperature": ffn("temperature"),
    }
    nc = _bacc.Bacc("TRN2", target_bir_lowering=False, num_devices=1)
    arrays, args = {}, []
    for name, value in given.items():
        a = _np.ascontiguousarray(value)
        arrays[f"in_{name}_dram"] = a
        args.append(nc.dram_tensor(f"in_{name}_dram", a.shape, _mybir.dt.from_np(a.dtype), kind="ExternalInput").ap())
    args.append(nc.dram_tensor("out_0_dram", (B, S, D), _mybir.dt.float32, kind="ExternalOutput").ap())
    xattn_ffn_kernel(nc, *args)
    r = _run(nc, [arrays], core_ids=[0])
    return r.results[0]["out_0_dram"]
```

```python
import math
from contextlib import ExitStack

import concourse.bass as bass
from concourse import mybir

B, S, D = 4, 512, 512
C = 128
E, F, R = 8, 512, 64
P = 128
KT = D // P
FT = F // P
TT = S // P
NBLK = B

FIRST_EXPERT, LAST_EXPERT = 0, 1
POSITIONS = E

UNIT_CREDIT = 2
BLOCK_CREDIT = 4

GOLDEN_CENTER = 1.0 / math.e
GOLDEN_LOWER = 0.5 - math.log(4.0 / 3.0)
Z_LOWER = math.log(GOLDEN_LOWER / (1.0 - GOLDEN_LOWER))
Z_UPPER = 2.0 ** -23
SCALE = 512.0 ** -0.5
LN_EPS = 1e-5
SIM_EPS = 1e-6

ROUTER_STEPS = 14
OUT_BANK = [0, 1]
SIM_BANK = [2, 3, 0, 1]
HALF = S // 2


def xattn_ffn_kernel(nc, x, ctxT, wkT, bk, gamma, beta, wg, wu, wd, loraT, lora, wr, temperature, out):
    fp32 = mybir.dt.float32
    f32r = mybir.dt.float32r
    ALU = mybir.AluOpType
    ACT = mybir.ActivationFunctionType
    AX = mybir.AxisListType

    with ExitStack() as ctx:
        def sb(name, shape, dt=fp32):
            return ctx.enter_context(nc.sbuf_tensor(name, shape, dt))

        def sem(name):
            return ctx.enter_context(nc.semaphore(name))

        xacc = sb("xacc", [P, B * TT * D])
        xT_hi = sb("xT_hi", [P, KT, B * S], f32r)
        xT_lo = sb("xT_lo", [P, KT, B * S], f32r)
        w_raw = sb("w_raw", [P, 3, 4, 512])
        w_hi = sb("w_hi", [P, 3, 4, 512], f32r)
        w_lo = sb("w_lo", [P, 3, 4, 512], f32r)
        mid_hi = sb("mid_hi", [P, FT, S], f32r)
        mid_lo = sb("mid_lo", [P, FT, S], f32r)
        silu = sb("silu", [P, 2, S])
        mid = sb("mid", [P, 2, S])
        zt = sb("zt", [P, TT, S])
        beta_sb = sb("beta_sb", [P, S])
        bk_col = sb("bk_col", [P, 1])
        wr_sb = sb("wr_sb", [P, KT, E])
        temp_sb = sb("temp_sb", [P, 1])
        inv_temp = sb("inv_temp", [P, 1])
        half_less_center = sb("half_less_center", [P, 1])
        neg_half = sb("neg_half", [P, TT])
        below = sb("below", [P, E, E], mybir.dt.bfloat16)
        bn = sb("bn", [P, TT, 6])
        mv1 = sb("mv1", [P, TT, 2])
        mv2 = sb("mv2", [P, TT, 2])
        mv3 = sb("mv3", [P, TT, 2])
        var = sb("var", [P, 3, TT])
        rstd = sb("rstd", [P, 3, TT])
        sim_rs = sb("sim_rs", [P, TT])
        negmax = sb("negmax", [P, TT])
        esum = sb("esum", [P, TT])
        rsum = sb("rsum", [P, TT])
        z = sb("z", [P, TT, E])
        dist = sb("dist", [P, TT, E])
        tanh_z = sb("tanh_z", [P, TT, E])
        w_zone = sb("w_zone", [P, TT, E])
        fb = sb("fb", [P, TT, E])
        rank = sb("rank", [P, TT, E])
        beats = sb("beats", [P, TT, E, E], mybir.dt.uint8)
        ties = sb("ties", [P, TT, E, E], mybir.dt.uint8)
        rsums = sb("rsums", [P, 2, TT])
        rw = sb("rw", [P, B * TT * E])

        def in_raw(first, n):
            return w_raw[:, :, :, :].rearrange("p m k c -> p (m k c)")[:, first * 512:(first + n) * 512]
        pT = in_raw(0, 4).rearrange("p (k i) -> p k i", k=4)
        kv = in_raw(4, 1).rearrange("p (j d) -> p j d", j=4)
        kvT = in_raw(5, 1)
        ctxT_sb = in_raw(6, 1)
        outT = in_raw(7, 1)
        xn = in_raw(8, 2).rearrange("p (u c) -> p u c", u=2)
        xn2 = [in_raw(8, 1), in_raw(9, 1), in_raw(4, 1), in_raw(5, 1)]

        bk_row = in_raw(10, 1)[:, 0:C]
        wkT_sb = in_raw(10, 1)[:, C:2 * C]
        ident = in_raw(10, 1)[:, 2 * C:2 * C + P]
        gamma_sb = in_raw(11, 1)

        tiles = ctx.enter_context(nc.psum_tensor("tiles", [P, 4, 512], fp32))
        gate_up = ctx.enter_context(nc.psum_tensor("gate_up", [P, 4, 512], fp32))

        wk_loaded = sem("wk_loaded")
        const_loaded = sem("const_loaded")
        consts_made = sem("consts_made")
        masks_made = sem("masks_made")
        inv_temp_made = sem("inv_temp_made")
        x_loaded = sem("x_loaded")
        ctx_loaded = sem("ctx_loaded")
        gu_loaded = sem("gu_loaded")
        d_loaded = sem("d_loaded")
        lora_loaded = sem("lora_loaded")
        lora_mm = sem("lora_mm")
        lora_added = sem("lora_added")
        w_hi_made = sem("w_hi_made")
        w_gu_ready = sem("w_gu_ready")
        w_d_ready = sem("w_d_ready")
        bn_done = [sem(f"bn_done{i}") for i in range(3)]
        mv_done = [sem(f"mv_done{i}") for i in range(3)]
        eps_set = [sem(f"eps_set{i}") for i in range(3)]
        var_ready = [sem(f"var_ready{i}") for i in range(3)]
        rstd_ready = [sem(f"rstd_ready{i}") for i in range(3)]
        xn_ready = sem("xn_ready")
        transposed = sem("transposed")
        kv_mm = sem("kv_mm")
        kv_ready = sem("kv_ready")
        kvT_ready = sem("kvT_ready")
        pT_ready = sem("pT_ready")
        out_mm = sem("out_mm")
        outT_ready = sem("outT_ready")
        sim_mm = sem("sim_mm")
        sim_rs_ready = sem("sim_rs_ready")
        sim_read = sem("sim_read")
        z_ready = sem("z_ready")
        max_ready = sem("max_ready")
        exp_done = sem("exp_done")
        rsum_ready = sem("rsum_ready")
        x2_ready = sem("x2_ready")
        x2nT_ready = sem("x2nT_ready")
        xT_hi_ready = sem("xT_hi_ready")
        xT_lo_ready = sem("xT_lo_ready")
        xT_lo_last = sem("xT_lo_last")
        logits_mm = sem("logits_mm")
        logits_read = sem("logits_read")
        router_act = sem("router_act")
        router_dve = sem("router_dve")
        rw_ready = sem("rw_ready")
        gu_mm = sem("gu_mm")
        silu_made = sem("silu_made")
        mid_made = sem("mid_made")
        hi_made = sem("hi_made")
        lo_made = sem("lo_made")
        down_mm = sem("down_mm")
        acc_done = sem("acc_done")
        stored = sem("stored")

        def reach(eng, s, count):
            if not isinstance(count, int) or count > 0:
                eng.wait_ge(s, count)

        def tile_of(a, t):
            return xacc[:, bass.ds((a * TT + t) * D, D)]

        def plain(ap):
            return ap.bitcast(fp32)

        def first_raw(m):
            return xacc[:, (1 + m) * TT * D:(2 + m) * TT * D].rearrange("p (k c) -> p k c", k=4)

        LORA_PARTS = [(0, 0), (64, 0), (0, 2)]

        def lora_slot(r, slot):
            if r:
                return zt[:, slot, :]
            return mid[:, slot, :] if slot < 2 else silu[:, slot - 2, :]

        block = ctx.enter_context(nc.Block())

        @block.sync
        def _(sp):
            def load_x(a):
                sp.dma_start(xacc[:, a * TT * D:(a + 1) * TT * D].rearrange("p (t c) -> p t c", t=TT),
                             x[a, :, :].rearrange("(t p) c -> p t c", p=P)).then_inc(x_loaded, 16)

            def load_gate_up(e):
                for m, w in enumerate((wg, wu)):
                    sp.dma_start(w_raw[:, m, :, :], w[bass.ds(e, 1), :, :].rearrange("o (k p) f -> p (o k) f", p=P))\
                      .then_inc(gu_loaded, 16)

            def load_down(e):
                sp.dma_start(w_raw[:, 2, :, :], wd[bass.ds(e, 1), :, :].rearrange("o (k p) f -> p (o k) f", p=P))\
                  .then_inc(d_loaded, 16)

            def load_lora(r, e):
                for m, (p0, slot) in enumerate(LORA_PARTS):
                    sp.dma_start(lora_slot(r, slot)[p0:p0 + R, :], loraT[m, e, :, :]).then_inc(lora_loaded, 16)
                    sp.dma_start(lora_slot(r, slot + 1)[p0:p0 + R, :], lora[m, e, :, :]).then_inc(lora_loaded, 16)

            sp.dma_start(ctxT_sb, ctxT[0, :, :]).then_inc(ctx_loaded, 16)
            load_x(0)
            load_lora(0, FIRST_EXPERT)
            for m, w in enumerate((wg, wu)):
                sp.dma_start(first_raw(m), w[FIRST_EXPERT, :, :].rearrange("(k p) f -> p k f", p=P)).then_inc(gu_loaded, 16)
            sp.dma_start(first_raw(2), wd[FIRST_EXPERT, :, :].rearrange("(k p) f -> p k f", p=P)).then_inc(d_loaded, 16)
            for a in range(1, B):
                sp.wait_ge(w_gu_ready, 4)
                if a == 3:
                    sp.wait_ge(w_d_ready, 1)
                sp.wait_ge(x_loaded, 16 * a)
                load_x(a)
                if a > 1:
                    sp.wait_ge(ctx_loaded, 16 * a)
                sp.wait_ge(kv_mm, a)
                sp.dma_start(ctxT_sb, ctxT[a, :, :]).then_inc(ctx_loaded, 16)

            sp.wait_ge(xT_lo_ready, B * (TT - 1))
            sp.wait_ge(xT_lo_last, B)
            sp.wait_ge(transposed, 8 * B)
            sp.wait_ge(logits_mm, B)
            load_gate_up(2)
            load_down(2)
            sp.wait_ge(x2_ready, B * TT)
            load_lora(1, LAST_EXPERT)
            with sp.Fori(2, POSITIONS - 1) as s:
                sp.wait_ge(w_gu_ready, s * 4)
                load_gate_up(s + 1)
                sp.wait_ge(w_d_ready, s)
                load_down(s + 1)
            sp.wait_ge(w_gu_ready, (POSITIONS - 1) * 4)
            load_gate_up(LAST_EXPERT)
            sp.wait_ge(w_d_ready, POSITIONS - 1)
            load_down(LAST_EXPERT)

            for i in range(B * TT):
                sp.wait_ge(acc_done, BLOCK_CREDIT + (POSITIONS - 1) * B * TT + i + 1)
                sp.dma_start(out[i // TT, (i % TT) * P:(i % TT + 1) * P, :], xacc[:, i * D:(i + 1) * D])\
                  .then_inc(stored, 16)
            sp.wait_ge(stored, 16 * B * TT)

        @block.gpsimd
        def _(pool):
            nc.gpsimd.memset(ident[:, :], 0.0).then_inc(consts_made, 1)
            nc.gpsimd.memset(below[:, :, :], 1.0).then_inc(consts_made, 1)
            nc.gpsimd.memset(neg_half[:, :], -0.5).then_inc(consts_made, 1)
            pool.wait_ge(consts_made, 3)
            nc.gpsimd.affine_select(out=ident[:, :], in_=ident[:, :], compare_op=ALU.not_equal, fill=1.0,
                                    base=0, pattern=[[-1, P]], channel_multiplier=1).then_inc(masks_made, 1)
            nc.gpsimd.affine_select(out=below[:, :, :], in_=below[:, :, :], compare_op=ALU.is_gt, fill=0.0,
                                    base=0, pattern=[[1, E], [-1, E]], channel_multiplier=0).then_inc(masks_made, 1)
            pool.sem_inc(lo_made, UNIT_CREDIT)

            def inverse_root(a, i):
                pool.wait_ge(var_ready[i], a + 1)
                nc.gpsimd.tensor_tensor(rstd[:, i, :], var[:, i, :], neg_half[:, :], ALU.pow)\
                  .then_inc(rstd_ready[i], 1)

            def low_part(n, f):
                pool.wait_ge(hi_made, n * FT + f + 1)
                pool.wait_ge(down_mm, n * TT + BLOCK_CREDIT)
                nc.gpsimd.tensor_tensor(mid_lo[:, f, :], mid[:, f % 2, :], plain(mid_hi[:, f, :]), ALU.subtract)\
                  .then_inc(lo_made, 1)

            def x_low_parts(a):
                for t in range(TT - 1):
                    pool.wait_ge(xT_hi_ready, a * TT + t + 1)
                    cols = bass.ds(a * S + t * P, P)
                    nc.gpsimd.tensor_tensor(xT_lo[:, :, cols], pT[:, :, t * P:(t + 1) * P],
                                            plain(xT_hi[:, :, cols]), ALU.subtract).then_inc(xT_lo_ready, 1)

            def first_gate_up_low_parts(pieces):
                for f in pieces:
                    cols = slice(f * P, (f + 1) * P)
                    pool.wait_ge(w_hi_made, f + 1)
                    for m in range(2):
                        ins = nc.gpsimd.tensor_tensor(w_lo[:, m, :, cols], first_raw(m)[:, :, cols],
                                                      plain(w_hi[:, m, :, cols]), ALU.subtract)
                    ins.then_inc(w_gu_ready, 1)

            def first_down_low_part():
                pool.wait_ge(w_hi_made, 5)
                nc.gpsimd.tensor_tensor(w_lo[:, 2, :, :], first_raw(2), plain(w_hi[:, 2, :, :]), ALU.subtract)\
                  .then_inc(w_d_ready, 1)

            inverse_root(0, 0)
            inverse_root(0, 1)
            first_gate_up_low_parts((0, 1))
            inverse_root(0, 2)
            first_gate_up_low_parts((2, 3))
            x_low_parts(0)
            first_down_low_part()
            with pool.Fori(0, B - 1) as n:
                inverse_root(n + 1, 0)
                low_part(n, 0)
                inverse_root(n + 1, 1)
                low_part(n, 1)
                low_part(n, 2)
                inverse_root(n + 1, 2)
                low_part(n, 3)
                x_low_parts(n + 1)
            with pool.Fori(B - 1, POSITIONS * NBLK) as n:
                for f in range(FT):
                    low_part(n, f)

        @block.scalar
        def _(act):
            act.dma_start(wkT_sb, wkT).then_inc(wk_loaded, 16)
            act.dma_start(bk_col[:, :], bk.rearrange("(d o) -> d o", o=1)).then_inc(wk_loaded, 16)
            act.dma_start(bk_row, bk.partition_broadcast(P)).then_inc(wk_loaded, 16)
            act.dma_start(gamma_sb[:, :], gamma.partition_broadcast(P)).then_inc(const_loaded, 16)
            act.dma_start(beta_sb[:, :], beta.partition_broadcast(P)).then_inc(const_loaded, 16)
            act.dma_start(wr_sb[:, :, :], wr.rearrange("(k p) e -> p k e", p=P)).then_inc(const_loaded, 16)
            act.dma_start(temp_sb[:, :], temperature.partition_broadcast(P)).then_inc(const_loaded, 16)

            def split_gate_up(g, f, src):
                cols = slice(f * P, (f + 1) * P)
                for m in range(2):
                    ins = nc.scalar.activation(w_hi[:, m, :, cols], src(m)[:, :, cols], ACT.Copy)
                ins.then_inc(w_hi_made, 1)

            def split_down(src):
                nc.scalar.activation(w_hi[:, 2, :, :], src(2), ACT.Copy).then_inc(w_hi_made, 1)

            def raw(m):
                return w_raw[:, m, :, :]

            def unit(n, f):
                act.wait_ge(gu_mm, n * FT + f + 1)
                act.wait_ge(mid_made, n * FT + f - 1 + UNIT_CREDIT)
                nc.scalar.activation(silu[:, f % 2, :], gate_up[:, 2 * (f % 2), :], ACT.Silu).then_inc(silu_made, 1)
                act.wait_ge(mid_made, n * FT + f + 1 + UNIT_CREDIT)
                act.wait_ge(down_mm, n * TT + BLOCK_CREDIT)
                nc.scalar.activation(mid_hi[:, f, :], mid[:, f % 2, :], ACT.Copy).then_inc(hi_made, 1)

            def kvT_bias(a):
                act.wait_ge(kv_mm, a + 1)
                nc.scalar.activation(kvT, gate_up[:, 3, :], ACT.Identity, bias=bk_col[:, 0:1]).then_inc(kvT_ready, 1)

            def copy_pT(a):
                for t in range(TT):
                    act.wait_ge(transposed, 8 * a + t + 1)
                    if t == 0:
                        reach(act, xT_lo_ready, a * (TT - 1))
                        reach(act, xT_lo_last, a)
                    nc.scalar.activation(pT[:, :, t * P:(t + 1) * P],
                                         tiles[:, t, :].rearrange("p (k i) -> p k i", k=KT), ACT.Copy)\
                      .then_inc(pT_ready, 1)

            def copy_outT(a):
                for h in range(2):
                    act.wait_ge(out_mm, 2 * a + h + 1)
                    nc.scalar.activation(outT[:, h * HALF:(h + 1) * HALF], tiles[:, OUT_BANK[h], 0:HALF], ACT.Copy)\
                      .then_inc(outT_ready, 1)

            def router_functions(a):
                act.wait_ge(logits_read, a + 1)
                nc.scalar.activation(tanh_z[:, :, :], z[:, :, :], ACT.Tanh, scale=0.5).then_inc(router_act, 1)
                act.wait_ge(router_act, 4 * a + 1)
                nc.scalar.activation(dist[:, :, :], tanh_z[:, :, :], ACT.Abs, scale=0.5, bias=half_less_center[:, 0:1])\
                  .then_inc(router_act, 1)
                act.wait_ge(router_act, 4 * a + 2)
                nc.scalar.activation(w_zone[:, :, :], dist[:, :, :], ACT.Exp, scale=-1.0 / 0.1).then_inc(router_act, 1)
                nc.scalar.activation(fb[:, :, :], dist[:, :, :], ACT.Exp, scale=-1.0 / 0.3).then_inc(router_act, 1)

            def exps(a):
                for t in range(TT):
                    act.wait_ge(max_ready, a * TT + t + 1)
                    nc.scalar.activation(zt[:, t, :], zt[:, t, :], ACT.Exp, bias=negmax[:, t:t + 1],
                                         accum_out=esum[:, t:t + 1]).then_inc(exp_done, 1)

            def copy_x2nT(a):
                for t in range(TT):
                    act.wait_ge(transposed, 8 * a + 4 + t + 1)
                    nc.scalar.activation(pT[:, :, t * P:(t + 1) * P],
                                         gate_up[:, t, :].rearrange("p (k i) -> p k i", k=KT), ACT.Copy)\
                      .then_inc(x2nT_ready, 1)
                    act.wait_ge(x2nT_ready, a * TT + t + 1)
                    nc.scalar.activation(xT_hi[:, :, bass.ds(a * S + t * P, P)], pT[:, :, t * P:(t + 1) * P], ACT.Copy)\
                      .then_inc(xT_hi_ready, 1)

            act.wait_ge(wk_loaded, 48)
            kvT_bias(0)
            copy_pT(0)
            copy_outT(0)
            exps(0)
            act.wait_ge(lora_added, 8)
            for f in range(FT):
                split_gate_up(0, f, first_raw)
            copy_x2nT(0)
            act.wait_ge(lora_added, 12)
            split_down(first_raw)
            with act.Fori(0, B - 1) as n:
                unit(n, 0)
                copy_pT(n + 1)
                kvT_bias(n + 1)
                router_functions(n)
                copy_outT(n + 1)
                unit(n, 1)
                exps(n + 1)
                unit(n, 2)
                unit(n, 3)
                copy_x2nT(n + 1)
            unit(B - 1, 0)
            router_functions(B - 1)
            unit(B - 1, 1)
            unit(B - 1, 2)
            act.wait_ge(gu_loaded, 64)
            for f in range(FT - 1):
                split_gate_up(1, f, raw)
            unit(B - 1, 3)
            split_gate_up(1, FT - 1, raw)
            act.wait_ge(down_mm, NBLK * TT + BLOCK_CREDIT)
            act.wait_ge(d_loaded, 32)
            split_down(raw)

            def expert(s, lora_count=0):
                with act.Fori(0, B - 1) as b:
                    for f in range(FT):
                        unit(s * NBLK + b, f)
                n = s * NBLK + B - 1
                for f in range(FT):
                    unit(n, f)
                    if f == 0:
                        act.wait_ge(gu_loaded, (s + 2) * 32)
                        reach(act, lora_added, lora_count)
                    split_gate_up(s + 1, f, raw)
                act.wait_ge(down_mm, (n + 1) * TT + BLOCK_CREDIT)
                act.wait_ge(d_loaded, (s + 2) * 16)
                split_down(raw)

            with act.Fori(1, POSITIONS - 2) as s:
                expert(s)
            expert(POSITIONS - 2, lora_count=24)
            with act.Fori((POSITIONS - 1) * NBLK, POSITIONS * NBLK) as n:
                for f in range(FT):
                    unit(n, f)

        @block.vector
        def _(dve):
            dve.sem_inc(mid_made, UNIT_CREDIT)
            dve.sem_inc(acc_done, BLOCK_CREDIT)
            nc.vector.memset(half_less_center[:, :], 0.5 - GOLDEN_CENTER).then_inc(inv_temp_made, 1)

            def set_eps(i, half, eps):
                nc.vector.memset(var[:, i, 2 * half:2 * half + 2], eps).then_inc(eps_set[i], 1)

            def spread(i, mv, a, scale, eps):
                dve.wait_ge(bn_done[i], (a + 1) * TT)
                set_eps(i, 1, eps)
                for t in range(TT):
                    nc.vector.bn_aggr(mv[:, t, :], bn[:, t, :]).then_inc(mv_done[i], 1)
                dve.wait_ge(eps_set[i], 2 * a + 2)
                dve.wait_ge(mv_done[i], (a + 1) * TT)
                nc.vector.scalar_tensor_tensor(var[:, i, :], mv[:, :, 1], scale, var[:, i, :], ALU.mult, ALU.add)\
                  .then_inc(var_ready[i], 1)

            def normalise(a, t, first):
                if first:
                    reach(dve, transposed, 8 * a + t - 1)
                i, mv, dst = (0, mv1, xn[:, t % 2, :]) if first else (2, mv3, xn2[t])
                nc.vector.tensor_scalar(dst, tile_of(a, t), mv[:, t, 0:1], rstd[:, i, t:t + 1],
                                        ALU.subtract, ALU.mult).then_inc(xn_ready, 1)

            def last_x_low_part(a):
                t = TT - 1
                dve.wait_ge(xT_hi_ready, a * TT + TT)
                cols = bass.ds(a * S + t * P, P)
                nc.vector.tensor_tensor(xT_lo[:, :, cols], pT[:, :, t * P:(t + 1) * P],
                                        plain(xT_hi[:, :, cols]), ALU.subtract).then_inc(xT_lo_last, 1)

            def ln1_stats(a):
                dve.wait_ge(x_loaded, 16 * a + 16)
                set_eps(0, 0, LN_EPS)
                for t in range(TT):
                    nc.vector.bn_stats(bn[:, t, :], tile_of(a, t)).then_inc(bn_done[0], 1)
                spread(0, mv1, a, 1.0, LN_EPS)

            def kv_bias(a):
                dve.wait_ge(kv_mm, a + 1)
                nc.vector.tensor_tensor(kv, gate_up[:, 2, :].rearrange("p (j d) -> p j d", j=4),
                                        bk_row[:, None, :].broadcast_to([P, 4, C]), ALU.add).then_inc(kv_ready, 1)

            def sim_scores(a):
                for t in range(TT):
                    dve.wait_ge(sim_mm, a * TT + t + 1)
                    if t == 0:
                        set_eps(1, 0, SIM_EPS)
                    nc.vector.bn_stats(bn[:, t, :], tiles[:, SIM_BANK[t], :]).then_inc(bn_done[1], 1)
                spread(1, mv2, a, SCALE * SCALE, SIM_EPS)
                for t in range(TT):
                    nc.vector.scalar_tensor_tensor(zt[:, t, :], tiles[:, SIM_BANK[t], :], mv2[:, t, 0:1], gamma_sb[:, :],
                                                   ALU.subtract, ALU.mult).then_inc(sim_read, 1)
                dve.wait_ge(rstd_ready[1], a + 1)
                nc.vector.tensor_scalar(sim_rs[:, :], rstd[:, 1, :], SCALE, None, ALU.mult).then_inc(sim_rs_ready, 1)

            def sim_norm(a, pair):
                dve.wait_ge(sim_rs_ready, a + 1)
                for t in pair:
                    dve.wait_ge(sim_read, a * TT + t + 1)
                    nc.vector.scalar_tensor_tensor(zt[:, t, :], zt[:, t, :], sim_rs[:, t:t + 1], beta_sb[:, :],
                                                   ALU.mult, ALU.add).then_inc(z_ready, 1)
                for t in pair:
                    dve.wait_ge(z_ready, a * TT + t + 1)
                    nc.vector.tensor_reduce(negmax[:, t:t + 1], zt[:, t, :], AX.X, ALU.max, negate=True)\
                      .then_inc(max_ready, 1)

            def add_attention(a):
                for t in range(TT):
                    dve.wait_ge(exp_done, a * TT + t + 1)
                    nc.vector.reciprocal(rsum[:, t:t + 1], esum[:, t:t + 1]).then_inc(rsum_ready, 1)
                    dve.wait_ge(rsum_ready, a * TT + t + 1)
                    nc.vector.scalar_tensor_tensor(tile_of(a, t), zt[:, t, :], rsum[:, t:t + 1], tile_of(a, t),
                                                   ALU.mult, ALU.add).then_inc(x2_ready, 1)

            def ln2_stats(a):
                dve.wait_ge(x2_ready, a * TT + TT)
                set_eps(2, 0, LN_EPS)
                for t in range(TT):
                    nc.vector.bn_stats(bn[:, t, :], tile_of(a, t)).then_inc(bn_done[2], 1)
                spread(2, mv3, a, 1.0, LN_EPS)

            def read_logits(a):
                dve.wait_ge(logits_mm, a + 1)
                nc.vector.tensor_scalar(z[:, :, :], gate_up[:, 3, 0:TT * E].rearrange("p (t e) -> p t e", t=TT),
                                        inv_temp[:, 0:1], None, ALU.mult).then_inc(logits_read, 1)

            def router(a):
                count = [0]

                def step(ins):
                    ins.then_inc(router_dve, 1)
                    count[0] += 1
                    dve.wait_ge(router_dve, a * ROUTER_STEPS + count[0])

                def over_experts(v):
                    return v[:, :, None].broadcast_to([P, TT, E])

                dve.wait_ge(logits_read, a + 1)
                dve.wait_ge(router_act, 4 * a + 4)
                step(nc.vector.scalar_tensor_tensor(w_zone[:, :, :], z[:, :, :], Z_LOWER, w_zone[:, :, :],
                                                    ALU.is_ge, ALU.mult))
                step(nc.vector.scalar_tensor_tensor(w_zone[:, :, :], z[:, :, :], Z_UPPER, w_zone[:, :, :],
                                                    ALU.is_le, ALU.mult))
                step(nc.vector.tensor_reduce(rsums[:, 0, :], w_zone[:, :, :], AX.X, ALU.add))
                mine = fb[:, :, :, None].broadcast_to([P, TT, E, E])
                other = fb[:, :, None, :].broadcast_to([P, TT, E, E])
                step(nc.vector.tensor_tensor(beats[:, :, :, :], other, mine, ALU.is_gt))
                step(nc.vector.tensor_tensor(ties[:, :, :, :], other, mine, ALU.is_equal))
                step(nc.vector.tensor_tensor(ties[:, :, :, :], ties[:, :, :, :],
                                             below[:, None, :, :].broadcast_to([P, TT, E, E]), ALU.mult))
                step(nc.vector.tensor_tensor(beats[:, :, :, :], beats[:, :, :, :], ties[:, :, :, :], ALU.add))
                step(nc.vector.tensor_reduce(rank[:, :, :], beats[:, :, :, :], AX.X, ALU.add))
                step(nc.vector.scalar_tensor_tensor(fb[:, :, :], rank[:, :, :], 2.0, fb[:, :, :], ALU.is_lt, ALU.mult))
                step(nc.vector.scalar_tensor_tensor(fb[:, :, :], over_experts(rsums[:, 0, :]), 1e-8, fb[:, :, :],
                                                    ALU.is_lt, ALU.mult))
                step(nc.vector.tensor_tensor(w_zone[:, :, :], w_zone[:, :, :], fb[:, :, :], ALU.add))
                step(nc.vector.tensor_reduce(rsums[:, 1, :], w_zone[:, :, :], AX.X, ALU.add))
                step(nc.vector.tensor_scalar(rsums[:, 1, :], rsums[:, 1, :], 1e-8, None, ALU.max))
                step(nc.vector.reciprocal(rsums[:, 1, :], rsums[:, 1, :]))
                assert count[0] == ROUTER_STEPS
                nc.vector.tensor_tensor(rw[:, bass.ds(a * TT * E, TT * E)].rearrange("p (t e) -> p t e", t=TT),
                                        w_zone[:, :, :], over_experts(rsums[:, 1, :]), ALU.mult).then_inc(rw_ready, 1)

            def unit(n, f):
                dve.wait_ge(silu_made, n * FT + f + 1)
                dve.wait_ge(lo_made, n * FT + f - 1 + UNIT_CREDIT)
                nc.vector.tensor_tensor(mid[:, f % 2, :], silu[:, f % 2, :], gate_up[:, 2 * (f % 2) + 1, :], ALU.mult)\
                  .then_inc(mid_made, 1)

            def accumulate(n, b, e):
                for t in range(TT):
                    dve.wait_ge(down_mm, n * TT + t + 1 + BLOCK_CREDIT)
                    nc.vector.scalar_tensor_tensor(tile_of(b, t), tiles[:, t, :],
                                                   rw[:, bass.ds((b * TT + t) * E + e, 1)], tile_of(b, t),
                                                   ALU.mult, ALU.add).then_inc(acc_done, 1)

            def split_gate_up(g, f, src):
                cols = slice(f * P, (f + 1) * P)
                dve.wait_ge(w_hi_made, g * 5 + f + 1)
                for m in range(2):
                    ins = nc.vector.tensor_tensor(w_lo[:, m, :, cols], src(m)[:, :, cols], plain(w_hi[:, m, :, cols]),
                                                  ALU.subtract)
                ins.then_inc(w_gu_ready, 1)

            def split_down(g, src):
                dve.wait_ge(w_hi_made, g * 5 + 5)
                nc.vector.tensor_tensor(w_lo[:, 2, :, :], src(2), plain(w_hi[:, 2, :, :]), ALU.subtract)\
                  .then_inc(w_d_ready, 1)

            def raw(m):
                return w_raw[:, m, :, :]

            def add_lora(r, banks, dst, m):
                for k in range(4):
                    dve.wait_ge(lora_mm, r * 12 + m * 4 + k + 1)
                    nc.vector.tensor_tensor(dst(m)[:, k, :], dst(m)[:, k, :], banks[:, k, :], ALU.add)\
                      .then_inc(lora_added, 1)

            ln1_stats(0)
            dve.wait_ge(rstd_ready[0], 1)
            normalise(0, 0, True)
            normalise(0, 1, True)
            dve.wait_ge(wk_loaded, 48)
            kv_bias(0)
            normalise(0, 2, True)
            normalise(0, 3, True)
            dve.wait_ge(gu_loaded, 32)
            add_lora(0, gate_up, first_raw, 0)
            dve.wait_ge(const_loaded, 64)
            sim_scores(0)
            sim_norm(0, (0, 1))
            sim_norm(0, (2, 3))
            add_lora(0, gate_up, first_raw, 1)
            add_attention(0)
            ln2_stats(0)
            nc.vector.reciprocal(inv_temp[:, :], temp_sb[:, :]).then_inc(inv_temp_made, 1)
            dve.wait_ge(rstd_ready[2], 1)
            for t in range(TT):
                normalise(0, t, False)
            dve.wait_ge(d_loaded, 16)
            add_lora(0, tiles, first_raw, 2)
            last_x_low_part(0)
            dve.wait_ge(inv_temp_made, 2)
            with dve.Fori(0, B - 1) as n:
                a = n + 1
                ln1_stats(a)
                read_logits(n)
                dve.wait_ge(rstd_ready[0], a + 1)
                normalise(a, 0, True)
                normalise(a, 1, True)
                unit(n, 0)
                normalise(a, 2, True)
                normalise(a, 3, True)
                kv_bias(a)
                router(n)
                sim_scores(a)
                sim_norm(a, (0, 1))
                unit(n, 1)
                sim_norm(a, (2, 3))
                add_attention(a)
                unit(n, 2)
                ln2_stats(a)
                unit(n, 3)
                dve.wait_ge(rstd_ready[2], a + 1)
                for t in range(TT):
                    normalise(a, t, False)
                dve.wait_ge(rw_ready, n + 1)
                accumulate(n, n, FIRST_EXPERT)
                last_x_low_part(a)
            read_logits(B - 1)
            unit(B - 1, 0)
            router(B - 1)
            unit(B - 1, 1)
            unit(B - 1, 2)
            for f in range(FT - 1):
                split_gate_up(1, f, raw)
            unit(B - 1, 3)
            split_gate_up(1, FT - 1, raw)
            dve.wait_ge(rw_ready, B)
            accumulate(B - 1, B - 1, FIRST_EXPERT)
            split_down(1, raw)

            def expert(s, e, with_lora=False):
                with dve.Fori(0, B - 1) as b:
                    for f in range(FT):
                        unit(s * NBLK + b, f)
                    accumulate(s * NBLK + b, b, e)
                n = s * NBLK + B - 1
                if with_lora:
                    dve.wait_ge(gu_loaded, POSITIONS * 32)
                    dve.wait_ge(d_loaded, POSITIONS * 16)
                    for m in range(3):
                        add_lora(1, tiles, raw, m)
                for f in range(FT):
                    unit(n, f)
                    split_gate_up(s + 1, f, raw)
                accumulate(n, B - 1, e)
                split_down(s + 1, raw)

            with dve.Fori(1, POSITIONS - 2) as s:
                expert(s, s + 1)
            expert(POSITIONS - 2, POSITIONS - 1, with_lora=True)
            with dve.Fori(0, B) as b:
                for f in range(FT):
                    unit((POSITIONS - 1) * NBLK + b, f)
                accumulate((POSITIONS - 1) * NBLK + b, b, LAST_EXPERT)

        @block.tensor
        def _(pe):
            pe.sem_inc(down_mm, BLOCK_CREDIT)

            def three_passes(dst, w_h, w_l, x_h, x_l, first, last):
                nc.tensor.matmul(dst, w_h, x_h, start=first, stop=False)
                nc.tensor.matmul(dst, w_h, x_l, start=False, stop=False)
                return nc.tensor.matmul(dst, w_l, x_h, start=False, stop=last)

            def project_context(a):
                pe.wait_ge(ctx_loaded, 16 * a + 16)
                reach(pe, mid_made, a * FT - FT + UNIT_CREDIT if not isinstance(a, int) else 0)
                reach(pe, logits_read, a)
                for j in range(4):
                    nc.tensor.matmul(gate_up[:, 2, j * C:(j + 1) * C], ctxT_sb[:, j * P:(j + 1) * P], wkT_sb,
                                     start=True, stop=True)
                nc.tensor.matmul(gate_up[:, 3, :], wkT_sb, ctxT_sb, start=True, stop=True).then_inc(kv_mm, 1)

            def transpose_tile(dst, src):
                for k in range(KT):
                    ins = nc.tensor.transpose(dst[:, k * P:(k + 1) * P], src[:, k * P:(k + 1) * P], ident[:, :])
                ins.then_inc(transposed, 1)

            def transpose_x(a):
                reach(pe, sim_read, a * TT)
                reach(pe, acc_done, a * TT)
                for t in range(TT):
                    pe.wait_ge(xn_ready, 8 * a + t + 1)
                    transpose_tile(tiles[:, t, :], xn[:, t % 2, :])

            def attend(a):
                pe.wait_ge(pT_ready, a * TT + TT)
                pe.wait_ge(kv_ready, a + 1)
                for h in range(2):
                    for j in range(4):
                        ins = nc.tensor.matmul(tiles[:, OUT_BANK[h], 0:HALF], kv[:, j, :],
                                               pT[:, j, h * HALF:(h + 1) * HALF], start=(j == 0), stop=(j == 3))
                    ins.then_inc(out_mm, 1)
                pe.wait_ge(kvT_ready, a + 1)
                for t in range(TT):
                    pe.wait_ge(outT_ready, 2 * a + (1 if t < 2 else 2))
                    nc.tensor.matmul(tiles[:, SIM_BANK[t], :], outT[:, t * P:(t + 1) * P], kvT, start=True, stop=True)\
                      .then_inc(sim_mm, 1)

            def transpose_x2(a):
                reach(pe, mid_made, a * FT + UNIT_CREDIT)
                for t in range(TT):
                    pe.wait_ge(xn_ready, 8 * a + 4 + t + 1)
                    transpose_tile(gate_up[:, t, :], xn2[t])

            def route(a):
                for t in range(TT):
                    pe.wait_ge(x2nT_ready, a * TT + (t + 1 if t else TT))
                    for k in range(KT):
                        ins = nc.tensor.matmul(gate_up[:, 3, t * E:(t + 1) * E], pT[:, k, t * P:(t + 1) * P], wr_sb[:, k, :],
                                               start=(k == 0), stop=(k == KT - 1))
                ins.then_inc(logits_mm, 1)

            def unit(n, b, f):
                pe.wait_ge(mid_made, n * FT + f - 1 + UNIT_CREDIT)
                p = f % 2
                for m in range(2):
                    for k in range(KT):
                        cols = slice(f * P, (f + 1) * P)
                        tok = bass.ds(b * S, S)
                        ins = three_passes(gate_up[:, 2 * p + m, :], w_hi[:, m, k, cols], w_lo[:, m, k, cols],
                                           xT_hi[:, k, tok], xT_lo[:, k, tok], k == 0, k == KT - 1)
                ins.then_inc(gu_mm, 1)

            def down(n, f):
                pe.wait_ge(lo_made, n * FT + f + 1 + UNIT_CREDIT)
                for t in range(TT):
                    if f == 0:
                        pe.wait_ge(acc_done, n * TT + t + 1)
                    toks = slice(t * P, (t + 1) * P)
                    ins = three_passes(tiles[:, t, :], mid_hi[:, f, toks], mid_lo[:, f, toks],
                                       w_hi[:, 2, f, :], w_lo[:, 2, f, :], f == 0, f == FT - 1)
                    if f == FT - 1:
                        ins.then_inc(down_mm, 1)

            def low_rank(r, banks, m, read=0):
                pe.wait_ge(lora_loaded, 96 * (r + 1))
                p0, slot = LORA_PARTS[m]
                for k in range(4):
                    reach(pe, lora_added, read + k + 1 if read else 0)
                    nc.tensor.matmul(banks[:, k, :], lora_slot(r, slot)[p0:p0 + R, k * P:(k + 1) * P],
                                     lora_slot(r, slot + 1)[p0:p0 + R, :], start=True, stop=True).then_inc(lora_mm, 1)

            pe.wait_ge(wk_loaded, 48)
            project_context(0)
            pe.wait_ge(masks_made, 2)
            transpose_x(0)
            pe.wait_ge(kv_ready, 1)
            pe.wait_ge(kvT_ready, 1)
            low_rank(0, gate_up, 0)
            attend(0)
            for k in range(4):
                pe.wait_ge(lora_added, k + 1)
            low_rank(0, gate_up, 1)
            pe.wait_ge(sim_read, TT)
            low_rank(0, tiles, 2)
            pe.wait_ge(lora_added, 8)
            transpose_x2(0)
            pe.wait_ge(const_loaded, 64)
            route(0)
            pe.wait_ge(w_gu_ready, 1)
            with pe.Fori(0, B - 1) as n:
                a = n + 1
                pe.wait_ge(xT_lo_ready, n * (TT - 1) + TT - 1)
                pe.wait_ge(xT_lo_last, n + 1)
                unit(n, n, 0)
                pe.wait_ge(lora_added, 12)
                transpose_x(a)
                project_context(a)
                attend(a)
                pe.wait_ge(w_gu_ready, 4)
                pe.wait_ge(kv_ready, a + 1)
                for f in range(1, FT):
                    unit(n, n, f)
                pe.wait_ge(w_d_ready, 1)
                pe.wait_ge(sim_read, a * TT + TT)
                down(n, 0)
                down(n, 1)
                transpose_x2(a)
                down(n, 2)
                down(n, 3)
                route(a)
            pe.wait_ge(xT_lo_ready, B * (TT - 1))
            pe.wait_ge(xT_lo_last, B)
            unit(B - 1, B - 1, 0)
            pe.wait_ge(logits_read, B)
            for f in range(1, FT):
                unit(B - 1, B - 1, f)
            for f in range(FT):
                down(B - 1, f)

            def blocks(s, first, end):
                with pe.Fori(first, end) as b:
                    n = s * NBLK + b
                    for f in range(FT):
                        pe.wait_ge(w_gu_ready, s * 4 + f + 1)
                        unit(n, b, f)
                    pe.wait_ge(w_d_ready, s + 1)
                    for f in range(FT):
                        down(n, f)

            with pe.Fori(1, POSITIONS - 2) as s:
                blocks(s, 0, B)
            blocks(POSITIONS - 2, 0, B - 1)
            pe.wait_ge(acc_done, ((POSITIONS - 2) * NBLK + B - 1) * TT + BLOCK_CREDIT)
            for m in range(3):
                low_rank(1, tiles, m, read=8 + 4 * m if m else 0)
            pe.wait_ge(lora_added, 24)
            blocks(POSITIONS - 2, B - 1, B)
            blocks(POSITIONS - 1, 0, B)


def kernel(**inputs):
    import numpy as _np
    import concourse.bacc as _bacc
    from concourse import mybir as _mybir
    from concourse.bass_utils import run_bass_kernel_spmd as _run

    def ffn(name):
        return _np.asarray(inputs["L0_ffn_" + name])

    given = {
        "x": inputs["x"],
        "ctxT": _np.asarray(inputs["ctx_512"]).transpose(0, 2, 1),
        "wkT": _np.asarray(inputs["L0_xattn_W_k"]).T,
        "bk": inputs["L0_xattn_b_k"],
        "gamma": inputs["L0_xattn_ln_gamma"],
        "beta": inputs["L0_xattn_ln_beta"],
        "wg": ffn("Wg"), "wu": ffn("Wu"), "wd": ffn("Wd"),
        "loraT": _np.stack([ffn(n).transpose(0, 2, 1) for n in ("Ga", "Ua", "Da")]),
        "lora": _np.stack([ffn(n) for n in ("Gb", "Ub", "Db")]),
        "wr": ffn("Wr"),
        "temperature": ffn("temperature"),
    }
    nc = _bacc.Bacc("TRN2", target_bir_lowering=False, num_devices=1)
    arrays, args = {}, []
    for name, value in given.items():
        a = _np.ascontiguousarray(value)
        arrays[f"in_{name}_dram"] = a
        args.append(nc.dram_tensor(f"in_{name}_dram", a.shape, _mybir.dt.from_np(a.dtype), kind="ExternalInput").ap())
    args.append(nc.dram_tensor("out_0_dram", (B, S, D), _mybir.dt.float32, kind="ExternalOutput").ap())
    xattn_ffn_kernel(nc, *args)
    r = _run(nc, [arrays], core_ids=[0])
    return r.results[0]["out_0_dram"]
```

```python
import math
from contextlib import ExitStack

import concourse.bass as bass
from concourse import mybir

B, S, D = 4, 512, 512
C = 128
E, F, R = 8, 512, 64
P = 128
KT = D // P
FT = F // P
TT = S // P
NBLK = B

LORA_EXPERTS = 2
POSITIONS = E
PLAIN = E - LORA_EXPERTS

PAIRS = ((0, 1), (2, 3))
FIRST_HALF = -1
EARLIER = FT

UNIT_CREDIT = 2
BLOCK_CREDIT = 4
LORA_CREDIT = 4

GOLDEN_CENTER = 1.0 / math.e
GOLDEN_LOWER = 0.5 - math.log(4.0 / 3.0)
Z_LOWER = math.log(GOLDEN_LOWER / (1.0 - GOLDEN_LOWER))
Z_UPPER = 2.0 ** -23
SCALE = 512.0 ** -0.5
LN_EPS = 1e-5
SIM_EPS = 1e-6

EPS_OF_VAR = SIM_EPS / SCALE ** 2

ROUTER_STEPS = 14
OUT_BANK = [0, 1]
SIM_BANK = [2, 3, 0, 1]
HALF = S // 2
FIRST, SECOND, WHOLE = slice(0, HALF), slice(HALF, S), slice(0, S)


def xattn_ffn_kernel(nc, x, xT, ctxT, wkT, bk, gamma, beta, wg, wu, wd, loraT, lora, wr, temperature, out):
    fp32 = mybir.dt.float32
    f32r = mybir.dt.float32r
    ALU = mybir.AluOpType
    ACT = mybir.ActivationFunctionType
    AX = mybir.AxisListType

    with ExitStack() as ctx:
        def sb(name, shape, dt=fp32):
            return ctx.enter_context(nc.sbuf_tensor(name, shape, dt))

        def sem(name):
            return ctx.enter_context(nc.semaphore(name))

        xacc = sb("xacc", [P, B * TT * D])
        xT_hi = sb("xT_hi", [P, KT, B * S], f32r)
        xT_lo_at = nc.sbuf_base
        xT_lo = sb("xT_lo", [P, KT, B * S], f32r)
        first_raw_all = nc.alloc_sbuf_tensor_at("first_raw_all", [P, KT, B * S], fp32, offset=xT_lo_at)
        w_raw = sb("w_raw", [P, 3, 4, 512])
        w_hi = sb("w_hi", [P, 3, 4, 512], f32r)
        w_lo = sb("w_lo", [P, 3, 4, 512], f32r)
        mid_hi = sb("mid_hi", [P, FT, S], f32r)
        mid_lo = sb("mid_lo", [P, FT, S], f32r)
        silu = sb("silu", [P, 2, S])
        mid = sb("mid", [P, 2, S])
        zt_at = nc.sbuf_base
        zt = sb("zt", [P, TT, S])
        lora_a, lora_b = (nc.alloc_sbuf_tensor_at(name, [P, S], fp32, offset=zt_at + i * S * 4)
                          for i, name in enumerate(("lora_a", "lora_b")))
        lora_a_split, lora_b_hi, lora_b_lo = (nc.alloc_sbuf_tensor_at(name, [P, S], f32r, offset=zt_at + i * S * 4)
                                              for name, i in (("lora_a_split", 2), ("lora_b_hi", 3), ("lora_b_lo", 1)))
        beta_sb = sb("beta_sb", [P, S])
        bk_col = sb("bk_col", [P, 1])
        wr_sb = sb("wr_sb", [P, KT, E])
        temp_sb = sb("temp_sb", [P, 1])
        inv_temp = sb("inv_temp", [P, 1])
        half_less_center = sb("half_less_center", [P, 1])
        neg_ctx_sum = sb("neg_ctx_sum", [P, 1])
        wr_split = sb("wr_split", [P, KT, 2 * E], f32r)
        fold = sb("fold", [2 * E, E])
        neg_half = sb("neg_half", [P, TT])
        below = sb("below", [P, E, E], mybir.dt.bfloat16)
        bn = sb("bn", [P, TT, 6])
        mv1 = sb("mv1", [P, TT, 2])
        mv2 = sb("mv2", [P, TT, 2])
        mv3 = sb("mv3", [P, TT, 2])
        var = sb("var", [P, 3, TT])
        rstd = sb("rstd", [P, 3, TT])
        negmax = sb("negmax", [P, TT])
        esum = sb("esum", [P, TT])
        rsum = sb("rsum", [P, TT])
        z = sb("z", [P, TT, E])
        dist = sb("dist", [P, TT, E])
        tanh_z = sb("tanh_z", [P, TT, E])
        w_zone = sb("w_zone", [P, TT, E])
        fb = sb("fb", [P, TT, E])
        rank = sb("rank", [P, TT, E])
        beats = sb("beats", [P, TT, E, E], mybir.dt.uint8)
        ties = sb("ties", [P, TT, E, E], mybir.dt.uint8)
        rsums = sb("rsums", [P, 2, TT])
        rw = sb("rw", [P, B * TT * E])

        def in_raw(first, n):
            return w_raw[:, :, :, :].rearrange("p m k c -> p (m k c)")[:, first * 512:(first + n) * 512]
        x_cols = in_raw(0, 4).rearrange("p (k i) -> p k i", k=4)
        kv = in_raw(4, 1).rearrange("p (j d) -> p j d", j=4)
        kvT = in_raw(5, 1)
        ctxT_sb = in_raw(6, 1)
        outT = in_raw(7, 1)
        logitsT = in_raw(8, 1)[0:2 * E, :]
        ctx_centered = in_raw(9, 1)
        xn = [x_cols[:, t, :] for t in range(TT)]

        wkT_sb = in_raw(10, 1)[:, 0:C]
        ident = in_raw(10, 1)[:, C:C + P]
        gamma_sb = in_raw(11, 1)

        tiles = ctx.enter_context(nc.psum_tensor("tiles", [P, 4, 512], fp32))
        gate_up = ctx.enter_context(nc.psum_tensor("gate_up", [P, 4, 512], fp32))

        wk_loaded = sem("wk_loaded")
        bk_loaded = sem("bk_loaded")
        const_loaded = sem("const_loaded")
        consts_made = sem("consts_made")
        masks_made = sem("masks_made")
        center_made = sem("center_made")
        wr_hi_made = sem("wr_hi_made")
        wr_split_done = sem("wr_split_done")
        xT_loaded = sem("xT_loaded")
        ctx_sum_made = sem("ctx_sum_made")
        ctx_centered_made = sem("ctx_centered_made")
        inv_temp_made = sem("inv_temp_made")
        x0_loaded = [sem(f"x0_loaded{t}") for t in range(TT)]
        x_loaded = sem("x_loaded")
        ctx_loaded = sem("ctx_loaded")
        gu_loaded = sem("gu_loaded")
        d_loaded = sem("d_loaded")
        lora_loaded = sem("lora_loaded")
        lora_hi = sem("lora_hi")
        lora_a_split_done = sem("lora_a_split_done")
        lora_b_split_done = sem("lora_b_split_done")
        lora_mm = sem("lora_mm")
        lora_added = sem("lora_added")
        w_hi_made = sem("w_hi_made")
        w_gu_ready = sem("w_gu_ready")
        w_d_ready = sem("w_d_ready")
        bn_done = [sem(f"bn_done{i}") for i in range(3)]
        mv_done = [sem(f"mv_done{i}") for i in range(3)]
        eps_set = [sem(f"eps_set{i}") for i in range(3)]
        var_ready = [sem(f"var_ready{i}") for i in range(3)]
        rstd_ready = [sem(f"rstd_ready{i}") for i in range(3)]
        xn_ready = sem("xn_ready")
        transposed = sem("transposed")
        kv_mm = sem("kv_mm")
        kv_ready = sem("kv_ready")
        kvT_ready = sem("kvT_ready")
        out_mm = sem("out_mm")
        outT_ready = sem("outT_ready")
        sim_mm = sem("sim_mm")
        sim_read = sem("sim_read")
        z_ready = sem("z_ready")
        max_ready = sem("max_ready")
        exp_done = sem("exp_done")
        rsum_ready = sem("rsum_ready")
        x2_ready = sem("x2_ready")
        xT_hi_ready = sem("xT_hi_ready")
        xT_lo_ready = sem("xT_lo_ready")
        logitsT_mm = sem("logitsT_mm")
        logitsT_read = sem("logitsT_read")
        logits_mm = sem("logits_mm")
        logits_read = sem("logits_read")
        router_act = sem("router_act")
        router_dve = sem("router_dve")
        rw_ready = sem("rw_ready")
        gu_mm = sem("gu_mm")
        silu_made = sem("silu_made")
        mid_made = sem("mid_made")
        hi_made = sem("hi_made")
        lo_made = sem("lo_made")
        down_mm = sem("down_mm")
        acc_done = sem("acc_done")
        stored = sem("stored")

        def reach(eng, s, count):
            if not isinstance(count, int) or count > 0:
                eng.wait_ge(s, count)

        def tile_of(a, t):
            return xacc[:, bass.ds((a * TT + t) * D, D)]

        def plain(ap):
            return ap.bitcast(fp32)

        def first_raw(m):
            return first_raw_all[:, :, (1 + m) * S:(2 + m) * S]

        block = ctx.enter_context(nc.Block())

        @block.sync
        def _(sp):
            def load_x(a):
                sp.dma_start(xacc[:, a * TT * D:(a + 1) * TT * D].rearrange("p (t c) -> p t c", t=TT),
                             x[a, :, :].rearrange("(t p) c -> p t c", p=P)).then_inc(x_loaded, 16)

            def load_gate_up(e):
                for m, w in enumerate((wg, wu)):
                    sp.dma_start(w_raw[:, m, :, :], w[bass.ds(e, 1), :, :].rearrange("o (k p) f -> p (o k) f", p=P))\
                      .then_inc(gu_loaded, 16)

            def load_down(e):
                sp.dma_start(w_raw[:, 2, :, :], wd[bass.ds(e, 1), :, :].rearrange("o (k p) f -> p (o k) f", p=P))\
                  .then_inc(d_loaded, 16)

            def load_position(g, e):
                sp.wait_ge(w_gu_ready, g * 4)
                load_gate_up(e)
                sp.wait_ge(w_d_ready, g)
                load_down(e)

            def load_lora(e, m):
                for rows in (slice(0, R), slice(R, 2 * R)):
                    sp.dma_start(lora_a[rows, :], loraT[bass.ds(m, 1), bass.ds(e, 1), :, :]
                                 .rearrange("m e r f -> (m e r) f")).then_inc(lora_loaded, 16)
                    sp.dma_start(lora_b[rows, :], lora[bass.ds(m, 1), bass.ds(e, 1), :, :]
                                 .rearrange("m e r f -> (m e r) f")).then_inc(lora_loaded, 16)

            def load_xT(a):
                sp.dma_start(x_cols, xT[a, :, :].rearrange("(k p) i -> p k i", p=P)).then_inc(xT_loaded, 16)

            def load_context(a):
                sp.dma_start(ctxT_sb, ctxT[a, :, :]).then_inc(ctx_loaded, 16)

            load_context(0)
            load_xT(0)
            for t in range(TT):
                sp.dma_start(xacc[:, t * D:(t + 1) * D], x[0, t * P:(t + 1) * P, :]).then_inc(x0_loaded[t], 16)
            sp.dma_start(gamma_sb[:, :], gamma.partition_broadcast(P)).then_inc(const_loaded, 16)
            sp.dma_start(beta_sb[:, :], beta.partition_broadcast(P)).then_inc(const_loaded, 16)
            sp.dma_start(wr_sb[:, :, :], wr.rearrange("(k p) e -> p k e", p=P)).then_inc(const_loaded, 16)
            sp.dma_start(temp_sb[:, :], temperature.partition_broadcast(P)).then_inc(const_loaded, 16)
            sp.wait_ge(kv_mm, 2)
            load_context(1)
            for m, w in enumerate((wg, wu)):
                sp.dma_start(first_raw(m), w[LORA_EXPERTS, :, :].rearrange("(k p) f -> p k f", p=P)).then_inc(gu_loaded, 16)
            sp.wait_ge(out_mm, 2)
            load_xT(1)
            sp.dma_start(first_raw(2), wd[LORA_EXPERTS, :, :].rearrange("(k p) f -> p k f", p=P)).then_inc(d_loaded, 16)
            for a in range(1, B):
                if a > 1:
                    sp.wait_ge(x_loaded, 16 * (a - 1))
                load_x(a)
            for a in range(2, B):
                sp.wait_ge(kv_mm, 2 * a)
                load_context(a)
                sp.wait_ge(transposed, (a - 1) * TT)
                load_xT(a)

            sp.wait_ge(transposed, B * TT)
            sp.wait_ge(logits_mm, B)
            load_gate_up(LORA_EXPERTS + 1)
            load_down(LORA_EXPERTS + 1)
            with sp.Fori(2, PLAIN) as g:
                load_position(g, g + LORA_EXPERTS)
            with sp.Fori(0, LORA_EXPERTS) as r:
                load_position(r + PLAIN, r)
                with sp.Fori(0, 3) as m:
                    sp.wait_ge(lora_mm, (r * 3 + m) * 4 + LORA_CREDIT)
                    load_lora(r, m)

            for i in range(B * TT):
                sp.wait_ge(acc_done, BLOCK_CREDIT + (POSITIONS - 1) * B * TT + i + 1)
                sp.dma_start(out[i // TT, (i % TT) * P:(i % TT + 1) * P, :], xacc[:, i * D:(i + 1) * D])\
                  .then_inc(stored, 16)
            sp.wait_ge(stored, 16 * B * TT)

        @block.gpsimd
        def _(pool):
            nc.gpsimd.memset(ident[:, :], 0.0).then_inc(consts_made, 1)
            nc.gpsimd.memset(below[:, :, :], 1.0).then_inc(consts_made, 1)
            nc.gpsimd.memset(neg_half[:, :], -0.5).then_inc(consts_made, 1)
            nc.gpsimd.memset(fold[:, :], 0.0).then_inc(consts_made, 1)
            pool.wait_ge(consts_made, 4)
            nc.gpsimd.affine_select(out=ident[:, :], in_=ident[:, :], compare_op=ALU.not_equal, fill=1.0,
                                    base=0, pattern=[[-1, P]], channel_multiplier=1).then_inc(masks_made, 1)
            nc.gpsimd.affine_select(out=below[:, :, :], in_=below[:, :, :], compare_op=ALU.is_gt, fill=0.0,
                                    base=0, pattern=[[1, E], [-1, E]], channel_multiplier=0).then_inc(masks_made, 1)
            for i in range(2):
                nc.gpsimd.affine_select(out=fold[:, :], in_=fold[:, :], compare_op=ALU.not_equal, fill=1.0,
                                        base=-i * E, pattern=[[-1, E]], channel_multiplier=1).then_inc(masks_made, 1)
                pool.wait_ge(masks_made, i + 3)
            pool.sem_inc(lo_made, UNIT_CREDIT)

            def inverse_root(a, i):
                pool.wait_ge(var_ready[i], a + 2)
                nc.gpsimd.tensor_tensor(rstd[:, i, :], var[:, i, :], neg_half[:, :], ALU.pow)\
                  .then_inc(rstd_ready[i], 1)

            def half_inverse_root(h, i):
                cols = slice(2 * h, 2 * h + 2)
                pool.wait_ge(var_ready[i], h + 1)
                nc.gpsimd.tensor_tensor(rstd[:, i, cols], var[:, i, cols], neg_half[:, cols], ALU.pow)\
                  .then_inc(rstd_ready[i], 1)

            def low_part(n, f, tokens=WHOLE):
                pool.wait_ge(hi_made, n * FT + f + 1 + EARLIER)
                if tokens == WHOLE:
                    pool.wait_ge(down_mm, n * TT + BLOCK_CREDIT)
                nc.gpsimd.tensor_tensor(mid_lo[:, f, tokens], mid[:, f % 2, tokens], plain(mid_hi[:, f, tokens]),
                                        ALU.subtract).then_inc(lo_made, 1)

            def first_gate_up_low_parts(pieces):
                for f in pieces:
                    cols = slice(f * P, (f + 1) * P)
                    pool.wait_ge(w_hi_made, f + 1)
                    for m in range(2):
                        ins = nc.gpsimd.tensor_tensor(w_lo[:, m, :, cols], first_raw(m)[:, :, cols],
                                                      plain(w_hi[:, m, :, cols]), ALU.subtract)
                    ins.then_inc(w_gu_ready, 1)

            def first_down_low_part(k):
                pool.wait_ge(w_hi_made, 5)
                ins = nc.gpsimd.tensor_tensor(w_lo[:, 2, k, :], first_raw(2)[:, k, :], plain(w_hi[:, 2, k, :]), ALU.subtract)
                if k == FT - 1:
                    ins.then_inc(w_d_ready, 1)

            def lora_b_low_part(q):
                pool.wait_ge(lora_hi, 2 * q + 2)
                nc.gpsimd.tensor_tensor(lora_b_lo[:, :], lora_b[:, :], plain(lora_b_hi[:, :]), ALU.subtract)\
                  .then_inc(lora_b_split_done, 1)

            half_inverse_root(0, 1)
            half_inverse_root(1, 1)
            first_gate_up_low_parts((0,))
            half_inverse_root(0, 2)
            first_gate_up_low_parts((1, 2, 3))
            for f in range(FT):
                low_part(FIRST_HALF, f, FIRST)
                if f == 0:
                    half_inverse_root(1, 2)
                first_down_low_part(f)

            def first_expert(n, tokens=WHOLE):
                low_part(n, 0, tokens)
                inverse_root(n + 1, 1)
                low_part(n, 1, tokens)
                low_part(n, 2, tokens)
                inverse_root(n + 1, 2)
                low_part(n, 3, tokens)

            first_expert(0, SECOND)
            with pool.Fori(1, B - 1) as n:
                first_expert(n)
            with pool.Fori(B - 1, (PLAIN - 1) * NBLK) as n:
                for f in range(FT):
                    low_part(n, f)
            with pool.Fori(0, LORA_EXPERTS) as r:
                with pool.Fori(0, 3) as m:
                    n = (r + PLAIN - 1) * NBLK + m
                    low_part(n, 0)
                    lora_b_low_part(r * 3 + m)
                    for f in range(1, FT):
                        low_part(n, f)
                for f in range(FT):
                    low_part((r + PLAIN) * NBLK - 1, f)
            with pool.Fori((POSITIONS - 1) * NBLK, POSITIONS * NBLK) as n:
                for f in range(FT):
                    low_part(n, f)

        @block.scalar
        def _(act):
            act.dma_start(wkT_sb, wkT).then_inc(wk_loaded, 16)
            act.dma_start(bk_col[:, :], bk.rearrange("(d o) -> d o", o=1)).then_inc(bk_loaded, 16)
            act.wait_ge(consts_made, 4)
            nc.scalar.activation(half_less_center[:, :], neg_half[:, 0:1], ACT.Copy, scale=2 * GOLDEN_CENTER - 1)\
              .then_inc(center_made, 1)

            def split_gate_up(g, f, src):
                cols = slice(f * P, (f + 1) * P)
                for m in range(2):
                    ins = nc.scalar.activation(w_hi[:, m, :, cols], src(m)[:, :, cols], ACT.Copy)
                ins.then_inc(w_hi_made, 1)

            def split_down(src):
                nc.scalar.activation(w_hi[:, 2, :, :], src(2), ACT.Copy).then_inc(w_hi_made, 1)

            def raw(m):
                return w_raw[:, m, :, :]

            def unit(n, f, tokens=WHOLE):
                u = n * FT + f + EARLIER
                act.wait_ge(gu_mm, u + 1)
                act.wait_ge(mid_made, u - 1 + UNIT_CREDIT)
                nc.scalar.activation(silu[:, f % 2, tokens], gate_up[:, 2 * (f % 2), tokens], ACT.Silu)\
                  .then_inc(silu_made, 1)
                act.wait_ge(mid_made, u + 1 + UNIT_CREDIT)
                if tokens == WHOLE:
                    act.wait_ge(down_mm, n * TT + BLOCK_CREDIT)
                nc.scalar.activation(mid_hi[:, f, tokens], mid[:, f % 2, tokens], ACT.Copy).then_inc(hi_made, 1)

            def center_context(a):
                act.wait_ge(ctx_sum_made, a + 1)
                reach(act, kv_mm, 2 * a)
                nc.scalar.activation(ctx_centered, ctxT_sb, ACT.Identity, scale=float(S), bias=neg_ctx_sum[:, 0:1])\
                  .then_inc(ctx_centered_made, 1)

            def copy_kv(a):
                act.wait_ge(kv_mm, 2 * a + 1)
                act.wait_ge(out_mm, 2 * a)
                nc.scalar.activation(kv, gate_up[:, 2, :].rearrange("p (j d) -> p j d", j=4), ACT.Copy, scale=1.0 / S)\
                  .then_inc(kv_ready, 1)

            def copy_kvT(a):
                act.wait_ge(kv_mm, 2 * a + 2)
                reach(act, sim_mm, a * TT)
                nc.scalar.activation(kvT, gate_up[:, 3, :], ACT.Identity, bias=bk_col[:, 0:1]).then_inc(kvT_ready, 1)

            def copy_outT(a, banks):
                for h in range(2):
                    act.wait_ge(out_mm, 2 * a + h + 1)
                    nc.scalar.activation(outT[:, h * HALF:(h + 1) * HALF], banks[:, OUT_BANK[h], 0:HALF], ACT.Copy)\
                      .then_inc(outT_ready, 1)

            def router_functions(a):
                act.wait_ge(logits_read, a + 1)
                nc.scalar.activation(tanh_z[:, :, :], z[:, :, :], ACT.Tanh, scale=0.5).then_inc(router_act, 1)
                act.wait_ge(router_act, 4 * a + 1)
                nc.scalar.activation(dist[:, :, :], tanh_z[:, :, :], ACT.Abs, scale=0.5, bias=half_less_center[:, 0:1])\
                  .then_inc(router_act, 1)
                act.wait_ge(router_act, 4 * a + 2)
                nc.scalar.activation(w_zone[:, :, :], dist[:, :, :], ACT.Exp, scale=-1.0 / 0.1).then_inc(router_act, 1)
                nc.scalar.activation(fb[:, :, :], dist[:, :, :], ACT.Exp, scale=-1.0 / 0.3).then_inc(router_act, 1)

            def exps(a, pair):
                for t in pair:
                    act.wait_ge(max_ready, a * TT + t + 1)
                    nc.scalar.activation(zt[:, t, :], zt[:, t, :], ACT.Exp, bias=negmax[:, t:t + 1],
                                         accum_out=esum[:, t:t + 1]).then_inc(exp_done, 1)

            def x_high_part(a, t, bank):
                act.wait_ge(transposed, a * TT + t + 1)
                nc.scalar.activation(xT_hi[:, :, bass.ds(a * S + t * P, P)],
                                     bank.rearrange("p (k i) -> p k i", k=KT), ACT.Copy).then_inc(xT_hi_ready, 1)

            def lora_high_parts(q):
                act.wait_ge(lora_loaded, 64 * q + 64)
                nc.scalar.activation(lora_a_split[:, :], lora_a[:, :], ACT.Copy).then_inc(lora_hi, 1)
                nc.scalar.activation(lora_b_hi[:, :], lora_b[:, :], ACT.Copy).then_inc(lora_hi, 1)

            act.wait_ge(bk_loaded, 16)
            copy_kvT(0)
            copy_outT(0, tiles)
            act.wait_ge(const_loaded, 64)
            nc.scalar.activation(wr_split[:, :, 0:E], wr_sb[:, :, :], ACT.Copy).then_inc(wr_hi_made, 1)
            center_context(1)
            copy_kv(1)
            copy_kvT(1)
            exps(0, PAIRS[0])
            act.wait_ge(gu_loaded, 32)
            for f in range(FT):
                split_gate_up(0, f, first_raw)
            copy_outT(1, gate_up)
            for t in PAIRS[0]:
                x_high_part(0, t, tiles[:, SIM_BANK[t], :])
            act.wait_ge(d_loaded, 16)
            split_down(first_raw)
            exps(0, PAIRS[1])
            for f in range(FT - 1):
                unit(FIRST_HALF, f, FIRST)
            for t in PAIRS[1]:
                x_high_part(0, t, tiles[:, SIM_BANK[t], :])
            unit(FIRST_HALF, FT - 1, FIRST)
            act.wait_ge(center_made, 1)
            def first_expert(n, more, tokens=WHOLE):
                if more:
                    center_context(n + 2)
                unit(n, 0, tokens)
                router_functions(n)
                unit(n, 1, tokens)
                if tokens == WHOLE:
                    exps(n + 1, PAIRS[0])
                if more:
                    copy_kv(n + 2)
                    copy_kvT(n + 2)
                if tokens == SECOND:
                    exps(n + 1, PAIRS[0])
                exps(n + 1, PAIRS[1])
                if more:
                    copy_outT(n + 2, tiles)
                unit(n, 2, tokens)
                unit(n, 3, tokens)
                for t in range(TT):
                    x_high_part(n + 1, t, gate_up[:, t, :])

            first_expert(0, True, SECOND)
            with act.Fori(1, B - 2) as n:
                first_expert(n, True)
            first_expert(B - 2, False)
            unit(B - 1, 0)
            unit(B - 1, 1)
            router_functions(B - 1)
            unit(B - 1, 2)
            act.wait_ge(gu_loaded, 64)
            for f in range(FT - 1):
                split_gate_up(1, f, raw)
            unit(B - 1, 3)
            split_gate_up(1, FT - 1, raw)
            act.wait_ge(down_mm, NBLK * TT + BLOCK_CREDIT)
            act.wait_ge(d_loaded, 32)
            split_down(raw)

            def last_block(s, lora_count=0):
                n = s * NBLK + B - 1
                for f in range(FT):
                    unit(n, f)
                    if f == 0:
                        act.wait_ge(gu_loaded, (s + 2) * 32)
                        reach(act, lora_added, lora_count)
                    split_gate_up(s + 1, f, raw)
                act.wait_ge(down_mm, (n + 1) * TT + BLOCK_CREDIT)
                act.wait_ge(d_loaded, (s + 2) * 16)
                split_down(raw)

            with act.Fori(1, PLAIN - 1) as s:
                with act.Fori(0, B - 1) as b:
                    for f in range(FT):
                        unit(s * NBLK + b, f)
                last_block(s)
            with act.Fori(0, LORA_EXPERTS) as r:
                with act.Fori(0, 3) as m:
                    n = (r + PLAIN - 1) * NBLK + m
                    unit(n, 0)
                    lora_high_parts(r * 3 + m)
                    for f in range(1, FT):
                        unit(n, f)
                last_block(r + PLAIN - 1, lora_count=(r + 1) * 12)
            with act.Fori((POSITIONS - 1) * NBLK, POSITIONS * NBLK) as n:
                for f in range(FT):
                    unit(n, f)

        @block.vector
        def _(dve):
            dve.sem_inc(mid_made, UNIT_CREDIT)
            dve.sem_inc(acc_done, BLOCK_CREDIT)

            def set_eps(i, half, eps):
                nc.vector.memset(var[:, i, 2 * half:2 * half + 2], eps).then_inc(eps_set[i], 1)

            def spread(i, mv, a, scale, eps, plus=None):
                dve.wait_ge(bn_done[i], (a + 1) * TT)
                set_eps(i, 1, eps)
                for t in range(TT):
                    nc.vector.bn_aggr(mv[:, t, :], bn[:, t, :]).then_inc(mv_done[i], 1)
                dve.wait_ge(eps_set[i], 2 * a + 2)
                dve.wait_ge(mv_done[i], (a + 1) * TT)
                nc.vector.scalar_tensor_tensor(var[:, i, :], mv[:, :, 1], scale, var[:, i if plus is None else plus, :],
                                               ALU.mult, ALU.add).then_inc(var_ready[i], 1)

            def normalise(a, t, out_after):
                if t == 0 and out_after:
                    dve.wait_ge(out_mm, 2 * a + 4)
                elif t == 0:
                    dve.wait_ge(transposed, a * TT)
                nc.vector.tensor_scalar(xn[t], tile_of(a, t), mv3[:, t, 0:1], rstd[:, 2, t:t + 1],
                                        ALU.subtract, ALU.mult).then_inc(xn_ready, 1)

            def x_low_part(a, t, bank):
                dve.wait_ge(xT_hi_ready, a * TT + t + 1)
                cols = bass.ds(a * S + t * P, P)
                nc.vector.tensor_tensor(xT_lo[:, :, cols], bank.rearrange("p (k i) -> p k i", k=KT),
                                        plain(xT_hi[:, :, cols]), ALU.subtract).then_inc(xT_lo_ready, 1)

            def half_stats(h, i, mv, scale, eps, source, plus=None):
                pair = slice(2 * h, 2 * h + 2)
                for t in PAIRS[h]:
                    dve.wait_ge(sim_mm if i == 1 else x2_ready, t + 1)
                    nc.vector.bn_stats(bn[:, t, :], source(t)).then_inc(bn_done[i], 1)
                dve.wait_ge(bn_done[i], 2 * h + 2)
                set_eps(i, h, eps)
                for t in PAIRS[h]:
                    nc.vector.bn_aggr(mv[:, t, :], bn[:, t, :]).then_inc(mv_done[i], 1)
                dve.wait_ge(eps_set[i], h + 1)
                dve.wait_ge(mv_done[i], 2 * h + 2)
                nc.vector.scalar_tensor_tensor(var[:, i, pair], mv[:, pair, 1], scale, var[:, i if plus is None else plus, pair],
                                               ALU.mult, ALU.add).then_inc(var_ready[i], 1)

            def context_sum(a):
                dve.wait_ge(ctx_loaded, 16 * a + 16)
                reach(dve, ctx_centered_made, a)
                nc.vector.tensor_reduce(neg_ctx_sum[:, :], ctxT_sb, AX.X, ALU.add, negate=True).then_inc(ctx_sum_made, 1)

            def x_stats(a):
                first = isinstance(a, int) and a == 0
                if not first:
                    dve.wait_ge(x_loaded, 16 * a)
                set_eps(0, 0, EPS_OF_VAR * LN_EPS)
                for t in range(TT):
                    if first:
                        dve.wait_ge(x0_loaded[t], 16)
                    nc.vector.bn_stats(bn[:, t, :], tile_of(a, t)).then_inc(bn_done[0], 1)
                spread(0, mv1, a, EPS_OF_VAR, EPS_OF_VAR * LN_EPS)

            def sim_scores(a, logits_of=None):
                for t in range(TT):
                    dve.wait_ge(sim_mm, a * TT + t + 1)
                    if t == 0:
                        dve.wait_ge(var_ready[0], a + 1)
                        set_eps(1, 0, 0.0)
                    if t == 1 and logits_of is not None:
                        read_logits(logits_of, gate_up)
                    nc.vector.bn_stats(bn[:, t, :], tiles[:, SIM_BANK[t], :]).then_inc(bn_done[1], 1)
                spread(1, mv2, a, 1.0, 0.0, plus=0)
                read_scores(range(TT))

            def read_scores(ts):
                for t in ts:
                    nc.vector.scalar_tensor_tensor(zt[:, t, :], tiles[:, SIM_BANK[t], :], mv2[:, t, 0:1], gamma_sb[:, :],
                                                   ALU.subtract, ALU.mult).then_inc(sim_read, 1)

            def sim_norm(a, pair, rstd_count=None):
                dve.wait_ge(rstd_ready[1], a + 2 if rstd_count is None else rstd_count)
                for t in pair:
                    dve.wait_ge(sim_read, a * TT + t + 1)
                    nc.vector.scalar_tensor_tensor(zt[:, t, :], zt[:, t, :], rstd[:, 1, t:t + 1], beta_sb[:, :],
                                                   ALU.mult, ALU.add).then_inc(z_ready, 1)

            def row_maxima(a, pair):
                for t in pair:
                    dve.wait_ge(z_ready, a * TT + t + 1)
                    nc.vector.tensor_reduce(negmax[:, t:t + 1], zt[:, t, :], AX.X, ALU.max, negate=True)\
                      .then_inc(max_ready, 1)

            def add_attention(a, ts=range(TT)):
                for t in ts:
                    dve.wait_ge(exp_done, a * TT + t + 1)
                    nc.vector.reciprocal(rsum[:, t:t + 1], esum[:, t:t + 1]).then_inc(rsum_ready, 1)
                    dve.wait_ge(rsum_ready, a * TT + t + 1)
                    nc.vector.scalar_tensor_tensor(tile_of(a, t), zt[:, t, :], rsum[:, t:t + 1], tile_of(a, t),
                                                   ALU.mult, ALU.add).then_inc(x2_ready, 1)

            def ln2_stats(a):
                dve.wait_ge(x2_ready, a * TT + TT)
                set_eps(2, 0, LN_EPS)
                for t in range(TT):
                    nc.vector.bn_stats(bn[:, t, :], tile_of(a, t)).then_inc(bn_done[2], 1)
                spread(2, mv3, a, 1.0, LN_EPS)

            def read_logitsT(a, banks):
                dve.wait_ge(logitsT_mm, a + 1)
                nc.vector.tensor_scalar(logitsT, banks[0:2 * E, 2, :], inv_temp[0:2 * E, 0:1], None, ALU.mult)\
                  .then_inc(logitsT_read, 1)

            def read_logits(a, banks):
                dve.wait_ge(logits_mm, a + 1)
                nc.vector.tensor_scalar(z[:, :, :], banks[:, 3, 0:TT * E].rearrange("p (t e) -> p t e", t=TT),
                                        1.0, None, ALU.mult).then_inc(logits_read, 1)

            def router(a):
                count = [0]

                def step(ins):
                    ins.then_inc(router_dve, 1)
                    count[0] += 1
                    dve.wait_ge(router_dve, a * ROUTER_STEPS + count[0])

                def over_experts(v):
                    return v[:, :, None].broadcast_to([P, TT, E])

                dve.wait_ge(logits_read, a + 1)
                dve.wait_ge(router_act, 4 * a + 4)
                step(nc.vector.scalar_tensor_tensor(w_zone[:, :, :], z[:, :, :], Z_LOWER, w_zone[:, :, :],
                                                    ALU.is_ge, ALU.mult))
                step(nc.vector.scalar_tensor_tensor(w_zone[:, :, :], z[:, :, :], Z_UPPER, w_zone[:, :, :],
                                                    ALU.is_le, ALU.mult))
                step(nc.vector.tensor_reduce(rsums[:, 0, :], w_zone[:, :, :], AX.X, ALU.add))
                mine = fb[:, :, :, None].broadcast_to([P, TT, E, E])
                other = fb[:, :, None, :].broadcast_to([P, TT, E, E])
                step(nc.vector.tensor_tensor(beats[:, :, :, :], other, mine, ALU.is_gt))
                step(nc.vector.tensor_tensor(ties[:, :, :, :], other, mine, ALU.is_equal))
                step(nc.vector.tensor_tensor(ties[:, :, :, :], ties[:, :, :, :],
                                             below[:, None, :, :].broadcast_to([P, TT, E, E]), ALU.mult))
                step(nc.vector.tensor_tensor(beats[:, :, :, :], beats[:, :, :, :], ties[:, :, :, :], ALU.add))
                step(nc.vector.tensor_reduce(rank[:, :, :], beats[:, :, :, :], AX.X, ALU.add))
                step(nc.vector.scalar_tensor_tensor(fb[:, :, :], rank[:, :, :], 2.0, fb[:, :, :], ALU.is_lt, ALU.mult))
                step(nc.vector.scalar_tensor_tensor(fb[:, :, :], over_experts(rsums[:, 0, :]), 1e-8, fb[:, :, :],
                                                    ALU.is_lt, ALU.mult))
                step(nc.vector.tensor_tensor(w_zone[:, :, :], w_zone[:, :, :], fb[:, :, :], ALU.add))
                step(nc.vector.tensor_reduce(rsums[:, 1, :], w_zone[:, :, :], AX.X, ALU.add))
                step(nc.vector.tensor_scalar(rsums[:, 1, :], rsums[:, 1, :], 1e-8, None, ALU.max))
                step(nc.vector.reciprocal(rsums[:, 1, :], rsums[:, 1, :]))
                assert count[0] == ROUTER_STEPS
                for first, last, to in ((LORA_EXPERTS, E, 0), (0, LORA_EXPERTS, PLAIN)):
                    ins = nc.vector.tensor_tensor(
                        rw[:, bass.ds(a * TT * E, TT * E)].rearrange("p (t e) -> p t e", t=TT)[:, :, to:to + last - first],
                        w_zone[:, :, first:last], rsums[:, 1, :, None].broadcast_to([P, TT, last - first]), ALU.mult)
                ins.then_inc(rw_ready, 1)

            def unit(n, f, tokens=WHOLE):
                u = n * FT + f + EARLIER
                dve.wait_ge(silu_made, u + 1)
                dve.wait_ge(lo_made, u - 1 + UNIT_CREDIT)
                nc.vector.tensor_tensor(mid[:, f % 2, tokens], silu[:, f % 2, tokens], gate_up[:, 2 * (f % 2) + 1, tokens],
                                        ALU.mult).then_inc(mid_made, 1)

            def accumulate(n, b, s):
                for t in range(TT):
                    dve.wait_ge(down_mm, n * TT + t + 1 + BLOCK_CREDIT)
                    nc.vector.scalar_tensor_tensor(tile_of(b, t), tiles[:, t, :],
                                                   rw[:, bass.ds((b * TT + t) * E + s, 1)], tile_of(b, t),
                                                   ALU.mult, ALU.add).then_inc(acc_done, 1)

            def split_gate_up(g, f, src):
                cols = slice(f * P, (f + 1) * P)
                dve.wait_ge(w_hi_made, g * 5 + f + 1)
                for m in range(2):
                    ins = nc.vector.tensor_tensor(w_lo[:, m, :, cols], src(m)[:, :, cols], plain(w_hi[:, m, :, cols]),
                                                  ALU.subtract)
                ins.then_inc(w_gu_ready, 1)

            def split_down(g, src):
                dve.wait_ge(w_hi_made, g * 5 + 5)
                nc.vector.tensor_tensor(w_lo[:, 2, :, :], src(2), plain(w_hi[:, 2, :, :]), ALU.subtract)\
                  .then_inc(w_d_ready, 1)

            def raw(m):
                return w_raw[:, m, :, :]

            def lora_a_low_part(q):
                dve.wait_ge(lora_hi, 2 * q + 2)
                nc.vector.tensor_tensor(lora_a_split[R:2 * R, :], lora_a[R:2 * R, :], plain(lora_a_split[R:2 * R, :]),
                                        ALU.subtract).then_inc(lora_a_split_done, 1)

            def add_lora(q, m, s):
                dve.wait_ge(gu_loaded, (s + 2) * 32)
                dve.wait_ge(d_loaded, (s + 2) * 16)
                for k in range(4):
                    dve.wait_ge(lora_mm, q * 4 + k + 1 + LORA_CREDIT)
                    part = w_raw[:, bass.ds(m, 1), k, :].rearrange("p o c -> p (o c)")
                    nc.vector.tensor_tensor(part, part, tiles[:, k, :], ALU.add).then_inc(lora_added, 1)

            context_sum(0)
            dve.wait_ge(ctx_sum_made, 1)
            nc.vector.tensor_scalar(ctx_centered, ctxT_sb, float(S), neg_ctx_sum[:, 0:1], ALU.mult, ALU.add)\
              .then_inc(ctx_centered_made, 1)
            dve.wait_ge(kv_mm, 1)
            nc.vector.tensor_scalar(kv, gate_up[:, 2, :].rearrange("p (j d) -> p j d", j=4), 1.0 / S, None, ALU.mult)\
              .then_inc(kv_ready, 1)
            x_stats(0)
            dve.wait_ge(const_loaded, 64)
            nc.vector.reciprocal(inv_temp[:, :], temp_sb[:, :]).then_inc(inv_temp_made, 1)
            context_sum(1)
            dve.wait_ge(wr_hi_made, 1)
            nc.vector.tensor_tensor(wr_split[:, :, E:2 * E], wr_sb[:, :, :], plain(wr_split[:, :, 0:E]), ALU.subtract)\
              .then_inc(wr_split_done, 1)
            def scores_of(t):
                return tiles[:, SIM_BANK[t], :]

            def x_of(t):
                return tile_of(0, t)

            dve.wait_ge(var_ready[0], 1)
            half_stats(0, 1, mv2, 1.0, 0.0, scores_of, plus=0)
            read_scores(PAIRS[0])
            sim_norm(0, PAIRS[0], 1)
            row_maxima(0, PAIRS[0])
            half_stats(1, 1, mv2, 1.0, 0.0, scores_of, plus=0)
            add_attention(0, PAIRS[0])
            half_stats(0, 2, mv3, 1.0, LN_EPS, x_of)
            read_scores(PAIRS[1])
            dve.wait_ge(rstd_ready[2], 1)
            for t in PAIRS[0]:
                normalise(0, t, True)
            sim_norm(0, PAIRS[1], 2)
            for t in PAIRS[0]:
                x_low_part(0, t, scores_of(t))
            row_maxima(0, PAIRS[1])
            add_attention(0, PAIRS[1])
            unit(FIRST_HALF, 0, FIRST)
            half_stats(1, 2, mv3, 1.0, LN_EPS, x_of)
            unit(FIRST_HALF, 1, FIRST)
            dve.wait_ge(rstd_ready[2], 2)
            for t in PAIRS[1]:
                normalise(0, t, True)
            unit(FIRST_HALF, 2, FIRST)
            for t in PAIRS[1]:
                x_low_part(0, t, scores_of(t))
            unit(FIRST_HALF, 3, FIRST)
            dve.wait_ge(inv_temp_made, 1)
            def first_expert(n, more, tokens=WHOLE):
                a = n + 1
                if more:
                    context_sum(a + 1)
                x_stats(a)
                unit(n, 0, tokens)
                read_logitsT(n, gate_up)
                sim_scores(a, logits_of=n)
                if tokens == SECOND:
                    unit(n, 1, tokens)
                sim_norm(a, PAIRS[0])
                row_maxima(a, PAIRS[0])
                if tokens == WHOLE:
                    unit(n, 1, tokens)
                sim_norm(a, PAIRS[1])
                row_maxima(a, PAIRS[1])
                add_attention(a)
                unit(n, 2, tokens)
                ln2_stats(a)
                unit(n, 3, tokens)
                dve.wait_ge(rstd_ready[2], a + 2)
                for t in range(TT):
                    normalise(a, t, more)
                dve.wait_ge(w_gu_ready, 4)
                dve.wait_ge(w_d_ready, 1)
                for t in range(TT):
                    x_low_part(a, t, gate_up[:, t, :])
                router(n)
                dve.wait_ge(rw_ready, n + 1)
                accumulate(n, n, 0)

            first_expert(0, True, SECOND)
            with dve.Fori(1, B - 2) as n:
                first_expert(n, True)
            first_expert(B - 2, False)
            unit(B - 1, 0)
            read_logitsT(B - 1, tiles)
            unit(B - 1, 1)
            read_logits(B - 1, tiles)
            router(B - 1)
            unit(B - 1, 2)
            for f in range(FT - 1):
                split_gate_up(1, f, raw)
            unit(B - 1, 3)
            split_gate_up(1, FT - 1, raw)
            dve.wait_ge(rw_ready, B)
            accumulate(B - 1, B - 1, 0)
            split_down(1, raw)

            def last_block(s):
                n = s * NBLK + B - 1
                for f in range(FT):
                    unit(n, f)
                    split_gate_up(s + 1, f, raw)
                accumulate(n, B - 1, s)
                split_down(s + 1, raw)

            with dve.Fori(1, PLAIN - 1) as s:
                with dve.Fori(0, B - 1) as b:
                    for f in range(FT):
                        unit(s * NBLK + b, f)
                    accumulate(s * NBLK + b, b, s)
                last_block(s)
            with dve.Fori(0, LORA_EXPERTS) as r:
                s = r + PLAIN - 1
                with dve.Fori(0, 3) as m:
                    n = s * NBLK + m
                    for f in range(FT):
                        if f == 3:
                            add_lora(r * 3 + m, m, s)
                        unit(n, f)
                        if f == 0:
                            lora_a_low_part(r * 3 + m)
                    accumulate(n, m, s)
                last_block(s)
            with dve.Fori(0, B) as b:
                for f in range(FT):
                    unit((POSITIONS - 1) * NBLK + b, f)
                accumulate((POSITIONS - 1) * NBLK + b, b, POSITIONS - 1)

        @block.tensor
        def _(pe):
            pe.sem_inc(down_mm, BLOCK_CREDIT)
            pe.sem_inc(lora_mm, LORA_CREDIT)

            def three_passes(dst, w_h, w_l, x_h, x_l, first, last):
                nc.tensor.matmul(dst, w_h, x_h, start=first, stop=False)
                nc.tensor.matmul(dst, w_h, x_l, start=False, stop=False)
                return nc.tensor.matmul(dst, w_l, x_h, start=False, stop=last)

            def project_kv(a):
                pe.wait_ge(ctx_centered_made, a + 1)
                for j in range(4):
                    ins = nc.tensor.matmul(gate_up[:, 2, j * C:(j + 1) * C], ctx_centered[:, j * P:(j + 1) * P], wkT_sb,
                                           start=True, stop=True)
                ins.then_inc(kv_mm, 1)

            def project_kvT(a):
                nc.tensor.matmul(gate_up[:, 3, :], wkT_sb, ctxT_sb, start=True, stop=True).then_inc(kv_mm, 1)

            def transpose_tile(dst, src):
                for k in range(KT):
                    ins = nc.tensor.transpose(dst[:, k * P:(k + 1) * P], src[:, k * P:(k + 1) * P], ident[:, :])
                ins.then_inc(transposed, 1)

            def x_times_kv(a, h, banks):
                pe.wait_ge(xT_loaded, 16 * a + 16)
                pe.wait_ge(kv_ready, a + 1)
                for j in range(4):
                    ins = nc.tensor.matmul(banks[:, OUT_BANK[h], 0:HALF], kv[:, j, :],
                                           x_cols[:, j, h * HALF:(h + 1) * HALF], start=(j == 0), stop=(j == 3))
                ins.then_inc(out_mm, 1)

            def scores(a, t):
                pe.wait_ge(kvT_ready, a + 1)
                pe.wait_ge(outT_ready, 2 * a + (1 if t < 2 else 2))
                nc.tensor.matmul(tiles[:, SIM_BANK[t], :], outT[:, t * P:(t + 1) * P], kvT, start=True, stop=True)\
                  .then_inc(sim_mm, 1)

            def transpose_x2(a, t, bank):
                pe.wait_ge(xn_ready, a * TT + t + 1)
                transpose_tile(bank, xn[t])

            def route(a, banks):
                tok = bass.ds(a * S, S)
                for k in range(KT):
                    nc.tensor.matmul(banks[0:2 * E, 2, :], wr_split[:, k, :], xT_hi[:, k, tok], start=(k == 0), stop=False)
                    ins = nc.tensor.matmul(banks[0:2 * E, 2, :], wr_split[:, k, :], xT_lo[:, k, tok], start=False,
                                           stop=(k == KT - 1))
                ins.then_inc(logitsT_mm, 1)

            def logits(a, banks):
                pe.wait_ge(logitsT_read, a + 1)
                for t in range(TT):
                    ins = nc.tensor.matmul(banks[:, 3, t * E:(t + 1) * E], logitsT[:, t * P:(t + 1) * P], fold[:, :],
                                           start=True, stop=True)
                ins.then_inc(logits_mm, 1)

            def unit(n, b, f, tokens=WHOLE, tiles_made=None):
                pe.wait_ge(mid_made, n * FT + f - 1 + EARLIER + UNIT_CREDIT)
                p = f % 2
                cols = slice(f * P, (f + 1) * P)
                tok = bass.ds(b * S + tokens.start, tokens.stop - tokens.start)
                if tiles_made is not None:
                    pe.wait_ge(xT_hi_ready, tiles_made)
                    reach(pe, xT_lo_ready, tiles_made - 2)
                for m in range(2):
                    dst = gate_up[:, 2 * p + m, tokens]
                    for k in range(KT):
                        nc.tensor.matmul(dst, w_hi[:, m, k, cols], xT_hi[:, k, tok], start=(k == 0), stop=False)
                        nc.tensor.matmul(dst, w_lo[:, m, k, cols], xT_hi[:, k, tok], start=False, stop=False)
                if tiles_made is not None:
                    pe.wait_ge(xT_lo_ready, tiles_made)
                for m in range(2):
                    for k in range(KT):
                        ins = nc.tensor.matmul(gate_up[:, 2 * p + m, tokens], w_hi[:, m, k, cols], xT_lo[:, k, tok],
                                               start=False, stop=(k == KT - 1))
                ins.then_inc(gu_mm, 1)

            def down(n, f):
                pe.wait_ge(lo_made, n * FT + f + 1 + EARLIER + UNIT_CREDIT)
                for t in range(TT):
                    if f == 0:
                        pe.wait_ge(acc_done, n * TT + t + 1)
                    toks = slice(t * P, (t + 1) * P)
                    ins = three_passes(tiles[:, t, :], mid_hi[:, f, toks], mid_lo[:, f, toks],
                                       w_hi[:, 2, f, :], w_lo[:, 2, f, :], f == 0, f == FT - 1)
                    if f == FT - 1:
                        ins.then_inc(down_mm, 1)

            def low_rank(q, n):
                pe.wait_ge(lora_a_split_done, q + 1)
                pe.wait_ge(lora_b_split_done, q + 1)
                pe.wait_ge(acc_done, n * TT + BLOCK_CREDIT)
                for k in range(4):
                    rows = slice(k * P, (k + 1) * P)
                    nc.tensor.matmul(tiles[:, k, :], lora_a_split[:, rows], lora_b_hi[:, :], start=True, stop=False)
                    nc.tensor.matmul(tiles[:, k, :], lora_a_split[:, rows], lora_b_lo[:, :], start=False, stop=True)\
                      .then_inc(lora_mm, 1)

            pe.wait_ge(wk_loaded, 16)
            pe.wait_ge(ctx_loaded, 16)
            project_kv(0)
            project_kvT(0)
            for h in range(2):
                x_times_kv(0, h, tiles)
            for t in range(TT):
                scores(0, t)
            project_kv(1)
            project_kvT(1)
            for h in range(2):
                x_times_kv(1, h, gate_up)
            pe.wait_ge(masks_made, 4)
            for t in PAIRS[0]:
                pe.wait_ge(sim_read, t + 1)
                transpose_x2(0, t, tiles[:, SIM_BANK[t], :])
            pe.wait_ge(outT_ready, 4)
            pe.wait_ge(kvT_ready, 2)
            for f in range(FT):
                pe.wait_ge(w_gu_ready, f + 1)
                if f == FT - 1:
                    for t in PAIRS[1]:
                        pe.wait_ge(sim_read, t + 1)
                        transpose_x2(0, t, tiles[:, SIM_BANK[t], :])
                unit(FIRST_HALF, 0, f, FIRST, 2 if f == 0 else None)
            def first_expert(n, more, tokens=WHOLE):
                a = n + 1
                unit(n, n, 0, tokens, n * TT + TT)
                pe.wait_ge(wr_split_done, 1)
                pe.wait_ge(mid_made, n * FT + EARLIER + UNIT_CREDIT)
                route(n, gate_up)
                pe.wait_ge(acc_done, n * TT + BLOCK_CREDIT)
                scores(a, 0)
                scores(a, 1)
                logits(n, gate_up)
                scores(a, 2)
                scores(a, 3)
                pe.wait_ge(logits_read, n + 1)
                unit(n, n, 1, tokens)
                unit(n, n, 2, tokens)
                if more:
                    pe.wait_ge(mid_made, n * FT + 2 + EARLIER + UNIT_CREDIT)
                    pe.wait_ge(ctx_loaded, 16 * a + 32)
                    project_kv(a + 1)
                    project_kvT(a + 1)
                    pe.wait_ge(sim_read, a * TT + TT)
                    for h in range(2):
                        x_times_kv(a + 1, h, tiles)
                    pe.wait_ge(kvT_ready, a + 2)
                unit(n, n, 3, tokens)
                if more:
                    pe.wait_ge(outT_ready, 2 * a + 4)
                pe.wait_ge(w_d_ready, 1)
                pe.wait_ge(sim_read, a * TT + TT)
                down(n, 0)
                down(n, 1)
                pe.wait_ge(mid_made, a * FT + EARLIER + UNIT_CREDIT)
                for t in range(TT):
                    transpose_x2(a, t, gate_up[:, t, :])
                down(n, 2)
                down(n, 3)

            first_expert(0, True, SECOND)
            with pe.Fori(1, B - 2) as n:
                first_expert(n, True)
            first_expert(B - 2, False)
            unit(B - 1, B - 1, 0, tiles_made=B * TT)
            pe.wait_ge(acc_done, (B - 1) * TT + BLOCK_CREDIT)
            route(B - 1, tiles)
            unit(B - 1, B - 1, 1)
            logits(B - 1, tiles)
            unit(B - 1, B - 1, 2)
            unit(B - 1, B - 1, 3)
            pe.wait_ge(logits_read, B)
            for f in range(FT):
                down(B - 1, f)

            def gate_and_up(s, b, f):
                pe.wait_ge(w_gu_ready, s * 4 + f + 1)
                unit(s * NBLK + b, b, f)

            def all_down(s, b):
                pe.wait_ge(w_d_ready, s + 1)
                for f in range(FT):
                    down(s * NBLK + b, f)

            with pe.Fori(1, PLAIN - 1) as s:
                with pe.Fori(0, B) as b:
                    for f in range(FT):
                        gate_and_up(s, b, f)
                    all_down(s, b)
            with pe.Fori(0, LORA_EXPERTS) as r:
                s = r + PLAIN - 1
                with pe.Fori(0, 3) as m:
                    for f in range(FT):
                        if f == 3:
                            low_rank(r * 3 + m, s * NBLK + m)
                        gate_and_up(s, m, f)
                    pe.wait_ge(lora_added, (r * 3 + m) * 4 + 4)
                    all_down(s, m)
                for f in range(FT):
                    gate_and_up(s, B - 1, f)
                all_down(s, B - 1)
            with pe.Fori(0, B) as b:
                for f in range(FT):
                    gate_and_up(POSITIONS - 1, b, f)
                all_down(POSITIONS - 1, b)


def kernel(**inputs):
    import numpy as _np
    import concourse.bacc as _bacc
    from concourse import mybir as _mybir
    from concourse.bass_utils import run_bass_kernel_spmd as _run

    def ffn(name):
        return _np.asarray(inputs["L0_ffn_" + name])

    given = {
        "x": inputs["x"],
        "xT": _np.asarray(inputs["x"]).transpose(0, 2, 1),
        "ctxT": _np.asarray(inputs["ctx_512"]).transpose(0, 2, 1),
        "wkT": _np.asarray(inputs["L0_xattn_W_k"]).T,
        "bk": inputs["L0_xattn_b_k"],
        "gamma": inputs["L0_xattn_ln_gamma"],
        "beta": inputs["L0_xattn_ln_beta"],
        "wg": ffn("Wg"), "wu": ffn("Wu"), "wd": ffn("Wd"),
        "loraT": _np.stack([ffn(n).transpose(0, 2, 1) for n in ("Ga", "Ua", "Da")]),
        "lora": _np.stack([ffn(n) for n in ("Gb", "Ub", "Db")]),
        "wr": ffn("Wr"),
        "temperature": ffn("temperature"),
    }
    nc = _bacc.Bacc("TRN2", target_bir_lowering=False, num_devices=1)
    arrays, args = {}, []
    for name, value in given.items():
        a = _np.ascontiguousarray(value)
        arrays[f"in_{name}_dram"] = a
        args.append(nc.dram_tensor(f"in_{name}_dram", a.shape, _mybir.dt.from_np(a.dtype), kind="ExternalInput").ap())
    args.append(nc.dram_tensor("out_0_dram", (B, S, D), _mybir.dt.float32, kind="ExternalOutput").ap())
    xattn_ffn_kernel(nc, *args)
    r = _run(nc, [arrays], core_ids=[0])
    return r.results[0]["out_0_dram"]
```
